# Optimizing a Trainium2 kernel written in Bass

```python
import numpy as np
import jax
import jax.numpy as jnp

def _softmax(x, axis=-1):
    return jax.nn.softmax(x, axis=axis)

def _gelu(x):
    return jax.nn.gelu(x, approximate=True)

def _silu(x):
    return jax.nn.silu(x)

def _sigmoid(x):
    return jax.nn.sigmoid(x)

def _layernorm(x, axis=-1, eps=1e-05):
    m = jnp.mean(x, axis=axis, keepdims=True)
    v = jnp.var(x, axis=axis, keepdims=True)
    return (x - m) / jnp.sqrt(v + eps)

def _scatter_add(tgt, idx, src, axis=0):
    return tgt.at[idx].add(src)

def _segment_sum(src, seg, n):
    return jax.ops.segment_sum(src, seg, n)
kernel_name = 'mk_dlrm_tower_d1_rec_r8_ba688a'

def setup_inputs(seed: int=0):
    np.random.seed(seed)
    _w = jnp.asarray

    def _rec_inputs():
        import jax
        import jax.numpy as jnp
        _tk = jax.random.key(seed)
        dense_ctx = jax.random.normal(jax.random.fold_in(_tk, 190), (2048, 16), jnp.float32)
        ids = jnp.stack([jax.random.randint(jax.random.fold_in(_tk, 200 + f), (2048,), 0, v, jnp.int32) for f, v in enumerate([1250, 1000, 1250, 12500, 1000, 1250, 12500, 1250])], axis=1)
        tbl_0 = 0.05 * jax.random.normal(jax.random.fold_in(_tk, 500 + 0), (1250, 1024), jnp.float32)
        tbl_1 = 0.05 * jax.random.normal(jax.random.fold_in(_tk, 500 + 1), (1000, 1024), jnp.float32)
        tbl_2 = 0.05 * jax.random.normal(jax.random.fold_in(_tk, 500 + 2), (1250, 1024), jnp.float32)
        tbl_3 = 0.05 * jax.random.normal(jax.random.fold_in(_tk, 500 + 3), (12500, 1024), jnp.float32)
        tbl_4 = 0.05 * jax.random.normal(jax.random.fold_in(_tk, 500 + 4), (1000, 1024), jnp.float32)
        tbl_5 = 0.05 * jax.random.normal(jax.random.fold_in(_tk, 500 + 5), (1250, 1024), jnp.float32)
        tbl_6 = 0.05 * jax.random.normal(jax.random.fold_in(_tk, 500 + 6), (12500, 1024), jnp.float32)
        tbl_7 = 0.05 * jax.random.normal(jax.random.fold_in(_tk, 500 + 7), (1250, 1024), jnp.float32)
        _rk = jax.random.fold_in(_tk, 7)
        W_top1 = 0.0310087 * jax.random.normal(jax.random.fold_in(_tk, 801), (1040, 512), jnp.float32)
        W_top2 = 0.0441942 * jax.random.normal(jax.random.fold_in(_tk, 802), (512, 256), jnp.float32)
        W_top3 = 0.0625 * jax.random.normal(jax.random.fold_in(_tk, 803), (256, 1), jnp.float32)
        b_top1 = jnp.zeros((512,), jnp.float32)
        b_top2 = jnp.zeros((256,), jnp.float32)
        return (dense_ctx, ids, tbl_0, tbl_1, tbl_2, tbl_3, tbl_4, tbl_5, tbl_6, tbl_7, W_top1, b_top1, W_top2, b_top2, W_top3)
    dense_ctx, ids, tbl_0, tbl_1, tbl_2, tbl_3, tbl_4, tbl_5, tbl_6, tbl_7, W_top1, b_top1, W_top2, b_top2, W_top3 = _rec_inputs()

    def _L0_rec_setup():
        import jax, jax.numpy as jnp
        import numpy as np
        B, F, H = (1024, 8, 1024)

        def _linear_params(key, fan_in, fan_out):
            kw, kb = jax.random.split(key)
            w = jax.random.normal(kw, (fan_in, fan_out), dtype=jnp.float32) * 0.02
            b = jax.random.normal(kb, (fan_out,), dtype=jnp.float32) * 0.02
            return (w, b)
        key = jax.random.key(seed)
        ks = jax.random.split(key, 7)
        field_vectors = jax.random.normal(ks[0], (B, F, H), dtype=jnp.float32)
        Wn1, bn1 = _linear_params(ks[1], H, H)
        Wn2, bn2 = _linear_params(ks[2], H, H)
        Wa1, ba1 = _linear_params(ks[3], 2 * H, H)
        Wa2, ba2 = _linear_params(ks[4], H, H)
        Wo1, bo1 = _linear_params(ks[5], 2 * H, H)
        Wo2, bo2 = _linear_params(ks[6], H, H)
        not_idx = jnp.array([2, 3], dtype=jnp.int64)
        and_pairs = jnp.array([[0, 1], [2, 3]], dtype=jnp.int64)
        or_pairs = jnp.array([[4, 5]], dtype=jnp.int64)
        return {'field_vectors': field_vectors, 'Wn1': Wn1, 'bn1': bn1, 'Wn2': Wn2, 'bn2': bn2, 'Wa1': Wa1, 'ba1': ba1, 'Wa2': Wa2, 'ba2': ba2, 'Wo1': Wo1, 'bo1': bo1, 'Wo2': Wo2, 'bo2': bo2, 'not_idx': not_idx, 'and_pairs': and_pairs, 'or_pairs': or_pairs}
    _L0_rec_all = _L0_rec_setup()
    _L0_rec_in = {k: v for k, v in _L0_rec_all.items() if k in ('Wn1', 'bn1', 'Wn2', 'bn2', 'Wa1', 'ba1', 'Wa2', 'ba2', 'Wo1', 'bo1', 'Wo2', 'bo2', 'not_idx', 'and_pairs', 'or_pairs')}
    del _L0_rec_all
    return {'dense_ctx': dense_ctx, 'ids': ids, 'tbl_0': tbl_0, 'tbl_1': tbl_1, 'tbl_2': tbl_2, 'tbl_3': tbl_3, 'tbl_4': tbl_4, 'tbl_5': tbl_5, 'tbl_6': tbl_6, 'tbl_7': tbl_7, 'W_top1': W_top1, 'b_top1': b_top1, 'W_top2': W_top2, 'b_top2': b_top2, 'W_top3': W_top3, 'L0_rec_Wn1': _L0_rec_in['Wn1'], 'L0_rec_bn1': _L0_rec_in['bn1'], 'L0_rec_Wn2': _L0_rec_in['Wn2'], 'L0_rec_bn2': _L0_rec_in['bn2'], 'L0_rec_Wa1': _L0_rec_in['Wa1'], 'L0_rec_ba1': _L0_rec_in['ba1'], 'L0_rec_Wa2': _L0_rec_in['Wa2'], 'L0_rec_ba2': _L0_rec_in['ba2'], 'L0_rec_Wo1': _L0_rec_in['Wo1'], 'L0_rec_bo1': _L0_rec_in['bo1'], 'L0_rec_Wo2': _L0_rec_in['Wo2'], 'L0_rec_bo2': _L0_rec_in['bo2'], 'L0_rec_not_idx': _L0_rec_in['not_idx'], 'L0_rec_and_pairs': _L0_rec_in['and_pairs'], 'L0_rec_or_pairs': _L0_rec_in['or_pairs']}

def reference(dense_ctx, ids, tbl_0, tbl_1, tbl_2, tbl_3, tbl_4, tbl_5, tbl_6, tbl_7, W_top1, b_top1, W_top2, b_top2, W_top3, L0_rec_Wn1, L0_rec_bn1, L0_rec_Wn2, L0_rec_bn2, L0_rec_Wa1, L0_rec_ba1, L0_rec_Wa2, L0_rec_ba2, L0_rec_Wo1, L0_rec_bo1, L0_rec_Wo2, L0_rec_bo2, L0_rec_not_idx, L0_rec_and_pairs, L0_rec_or_pairs):
    import jax
    import jax.numpy as jnp

    def _L0_rec_ref(field_vectors, Wn1, bn1, Wn2, bn2, Wa1, ba1, Wa2, ba2, Wo1, bo1, Wo2, bo2, not_idx, and_pairs, or_pairs):
        import jax, jax.numpy as jnp
        import numpy as np
        B, F, H = (1024, 8, 1024)

        def _linear_params(key, fan_in, fan_out):
            kw, kb = jax.random.split(key)
            w = jax.random.normal(kw, (fan_in, fan_out), dtype=jnp.float32) * 0.02
            b = jax.random.normal(kb, (fan_out,), dtype=jnp.float32) * 0.02
            return (w, b)
        num_fields = field_vectors.shape[1]
        x_not = jnp.take(field_vectors, not_idx, axis=1)
        t = jnp.tanh(jax.nn.relu(x_not @ Wn1 + bn1) @ Wn2 + bn2)
        iv = field_vectors.at[:, not_idx, :].set(t)

        def pair_fuse(pairs, W1, b1, W2, b2):
            v = jnp.concatenate([jnp.take(iv, pairs[:, 0], axis=1), jnp.take(iv, pairs[:, 1], axis=1)], axis=-1)
            return jax.nn.relu(v @ W1 + b1) @ W2 + b2
        and_out = pair_fuse(and_pairs, Wa1, ba1, Wa2, ba2)
        or_out = pair_fuse(or_pairs, Wo1, bo1, Wo2, bo2)
        processed = jnp.zeros((num_fields,), dtype=field_vectors.dtype).at[and_pairs.reshape(-1)].set(1.0).at[or_pairs.reshape(-1)].set(1.0)
        remaining = 1.0 - processed
        sum_res = and_out.sum(axis=1) + or_out.sum(axis=1) + jnp.einsum('bfh,f->bh', iv, remaining)
        count = and_pairs.shape[0] + or_pairs.shape[0] + remaining.sum()
        return sum_res / count
    e = jnp.stack([tbl_0[ids[:, 0]], tbl_1[ids[:, 1]], tbl_2[ids[:, 2]], tbl_3[ids[:, 3]], tbl_4[ids[:, 4]], tbl_5[ids[:, 5]], tbl_6[ids[:, 6]], tbl_7[ids[:, 7]]], axis=1)
    z = _L0_rec_ref(e, L0_rec_Wn1, L0_rec_bn1, L0_rec_Wn2, L0_rec_bn2, L0_rec_Wa1, L0_rec_ba1, L0_rec_Wa2, L0_rec_ba2, L0_rec_Wo1, L0_rec_bo1, L0_rec_Wo2, L0_rec_bo2, L0_rec_not_idx, L0_rec_and_pairs, L0_rec_or_pairs)
    z = z.reshape(z.shape[0], -1)
    h = jnp.concatenate([z, dense_ctx], axis=1)
    h = jnp.maximum(h @ W_top1 + b_top1, 0.0)
    h = jnp.maximum(h @ W_top2 + b_top2, 0.0)
    y = h @ W_top3
    return y

_drawn_inputs = setup_inputs


def setup_inputs(seed=0):
    import zlib

    import numpy as np

    out = dict(_drawn_inputs(seed))
    spreads = {'b_top1': (0.0, 0.1), 'b_top2': (0.0, 0.1)}
    factors = {'tbl_0': 4.572,
     'tbl_1': 4.535,
     'tbl_2': 8.0,
     'tbl_3': 8.0,
     'tbl_4': 4.707,
     'tbl_5': 4.577,
     'L0_rec_Wn1': 8.0,
     'L0_rec_bn1': 8.0,
     'L0_rec_Wn2': 8.0,
     'L0_rec_bn2': 8.0,
     'L0_rec_Wa1': 2.977,
     'L0_rec_ba1': 4.05,
     'L0_rec_Wo1': 3.476,
     'L0_rec_bo1': 8.0,
     'L0_rec_Wo2': 2.864}
    for name, (base, spread) in spreads.items():
        noise = np.random.default_rng([zlib.crc32(name.encode()), seed]).standard_normal(out[name].shape)
        drawn = base * np.exp(spread * noise) if base else spread * noise
        out[name] = jnp.asarray(drawn.astype(out[name].dtype))
    for name, factor in factors.items():
        out[name] = (out[name] * factor).astype(out[name].dtype)
    return out
```

```python
import numpy as np

import concourse.bass as bass
from concourse import mybir

B, F, H = 2048, 8, 1024
D, M1, M2 = 16, 512, 256
TABLE_ROWS = [1250, 1000, 1250, 12500, 1000, 1250, 12500, 1250]
TABLE_START = [sum(TABLE_ROWS[:f]) for f in range(F)]
ALL_ROWS = sum(TABLE_ROWS)
NOTS, AND_PAIRS, OR_PAIRS = 2, 2, 1
P = 128
KT = H // P
MT1, MT2 = M1 // P, M2 // P
BLOCK = 512
BLOCKS = B // BLOCK
RT = BLOCK // P
TILES = B // P
HALF = H // 2

SLOTS = 2 * (AND_PAIRS + OR_PAIRS)
C_NOT = 0
C_PX = C_NOT + NOTS
C_PT = C_PX + SLOTS
C_RX = C_PT + SLOTS
C_RT = C_RX + F
COLS = C_RT + NOTS
SKIP = 1 << 20

K_FIELD, K_START, K_LAST, K_ROW, K_IDENT = 0, F, 2 * F, 3 * F, 3 * F + TILES
K_COLS = K_IDENT + P
S_N1, S_A1, S_O1, S_A2, S_O2 = 0, KT, 2 * KT, 3 * KT, 4 * KT
S_T1 = 5 * KT
S_T2 = S_T1 + MT1
S_W3 = S_T2 + MT2
S_COLS = S_W3 + MT2

RING = 4
G_FOLD = 2 * KT
G_NOT = NOTS * 2 * KT
G_AND = AND_PAIRS * KT + MT1
G_OR = KT + MT1
G0_NOT = G_FOLD
G0_AND = G0_NOT + BLOCKS * G_NOT
G0_OR = G0_AND + BLOCKS * G_AND
R_NOT, R_AND, R_OR = NOTS * RT, 2 * AND_PAIRS * RT, 3 * RT
R0_NOT = RT
R0_AND = R0_NOT + BLOCKS * R_NOT + 2 * RT
R0_OR = R0_AND + BLOCKS * R_AND + 2 * RT
R_PRIME = 2 * RT
T_OR = MT1 + MT2 + 1
REM = F + NOTS
T_STORES = 16 * (1 + BLOCKS * NOTS * RT // 2)


def build(nc, table, ids, fields, consts, smalls, bn2, wn1, wn2, wa1, wo1, w2ta, w2to, wt1, wt1d,
          wt2, dense_t, out):
    fp32, i32 = mybir.dt.float32, mybir.dt.int32
    ALU, ACT, AX = mybir.AluOpType, mybir.ActivationFunctionType, mybir.AxisListType
    from contextlib import ExitStack

    ctx = ExitStack()
    with ctx:
        def sb(name, shape, dt=fp32):
            return ctx.enter_context(nc.sbuf_tensor(name, shape, dt))

        def sem(name):
            return ctx.enter_context(nc.semaphore(name))

        t_rows = nc.dram_tensor("t_rows", (NOTS * B, H), fp32, kind="Internal").ap()
        fo_dram = nc.dram_tensor("fo_dram", (P, KT * M1), fp32, kind="Internal").ap()
        and_dram = nc.dram_tensor("and_dram", (BLOCKS * P, MT1 * BLOCK), fp32, kind="Internal").ap()

        token = nc.dram_tensor("token", (4, P), fp32, kind="Internal").ap()

        W = sb("W", [P, 16, H])
        X = sb("X", [P, 4, KT, BLOCK])
        Hb = sb("Hb", [P, KT, BLOCK])
        Fw = sb("Fw", [P, KT, M1])
        Wt = sb("Wt", [P, KT, M1])
        rows = sb("rows", [P, 2, H])
        acc = sb("acc", [P, MT1, BLOCK])
        tmp = sb("tmp", [P, 2, BLOCK])
        wt2s = sb("wt2s", [P, MT1, M2])
        wt1ds = sb("wt1ds", [D, M1])
        dens = sb("dens", [D, BLOCK])
        cst = sb("cst", [P, K_COLS])
        small = sb("small", [P, S_COLS])
        bvec = sb("bvec", [P, KT])
        c1 = sb("c1", [P, MT1])
        invc = sb("invc", [P, 1])
        idx = sb("idx", [P, TILES + RT, COLS], i32)
        stage = sb("stage", [P, 2, RT, COLS], i32)
        ident = cst[:, K_IDENT:K_IDENT + P]
        Wf = W[:, :, :]
        fold_w = X[:, 1, :, :].rearrange("p k n -> p (k n)").rearrange("p (s k m) -> p s k m", s=RING, k=KT)
        not_rows = X[:, 2:4, :, :].rearrange("p s k n -> p (s k n)").rearrange("p (s n) -> p s n", n=H)
        rem_area = X[:, 3, :, :].rearrange("p k n -> p (k n)").rearrange("p (s n) -> p s n", n=H)
        rem_in, rem_sum = rem_area[:, 0:3, :], rem_area[:, 3, :]
        t_out = acc[:, :, :].rearrange("p m n -> p (m n)").rearrange("p (s n) -> p s n", n=H)
        scr = W[:, 15, :]

        mm = ctx.enter_context(nc.psum_tensor("mm", [P, RING, BLOCK], fp32))
        tp = ctx.enter_context(nc.psum_tensor("tp", [P, 2, BLOCK], fp32))
        tl = ctx.enter_context(nc.psum_tensor("tl", [P, 2, BLOCK], fp32))
        bnb = rows[:, 0, :]

        consts_in, smalls_in, ints_in = sem("consts_in"), sem("smalls_in"), sem("ints_in")
        bn2_in, wt_in = sem("bn2_in"), sem("wt_in")
        fold_in = [sem(f"fold_in{s}") for s in range(RING)]
        fo_out = [sem(f"fo_out{s}") for s in range(RING)]
        fo_in = sem("fo_in")
        wn1_in, wn2_in = sem("wn1_in"), sem("wn2_in")
        slice_in = [sem(f"slice_in{m}") for m in range(KT)]
        top_in, dense_in, and_in, and_out = sem("top_in"), sem("dense_in"), sem("and_in"), sem("and_out")
        t_stored = [sem(f"t_stored{s}") for s in range(2)]
        y_out = sem("y_out")
        setup = sem("setup")
        idx_ready, bvec_ready = sem("idx_ready"), sem("bvec_ready")
        staged, pool_holds = sem("staged"), sem("pool_holds")
        not_in = [sem(f"not_in{s}") for s in range(2 * RT)]
        x_in = [sem(f"x_in{s}") for s in range(2)]
        row_in = [sem(f"row_in{s}") for s in range(2)]
        zeroed = sem("zeroed")
        rem_got = [sem(f"rem_got{s}") for s in range(3)]
        rem_added, rem_summed = sem("rem_added"), sem("rem_summed")
        mm_full = sem("mm_full")
        act_freed = sem("act_freed")
        dve_freed = sem("dve_freed")
        biased = sem("biased")
        summed = sem("summed")
        turned = [sem("turned_a"), sem("turned_b")]
        taken = [sem("taken_a"), sem("taken_b")]
        tl_full, tl_freed = sem("tl_full"), sem("tl_freed")
        h1_ready, h2_ready = sem("h1_ready"), sem("h2_ready")
        c1_ready, y_ready = sem("c1_ready"), sem("y_ready")
        acc_step = sem("acc_step")

        block = ctx.enter_context(nc.Block())

        @block.sync
        def _(sp):
            def store_fold(sp, n):
                sp.wait_ge(act_freed, n + 1)
                sp.dma_start(fo_dram[:, (n - KT) * M1:(n - KT + 1) * M1], acc[:, n % RING, :]).then_inc(fo_out[n % RING], 16)

            sp.dma_start(cst[:, :], consts).then_inc(consts_in, 16)
            for n, s in enumerate(t_stored + [and_out, y_out]):
                sp.dma_start(token[n:n + 1, :], consts[0:1, 0:P]).then_inc(s, 16)
            sp.dma_start(scr[:, 0:TILES * F].bitcast(i32), ids).then_inc(ints_in, 16)
            sp.dma_start(scr[:, TILES * F:TILES * F + F].bitcast(i32),
                         fields.partition_broadcast(P)).then_inc(ints_in, 16)
            sp.dma_start(small[:, :], smalls).then_inc(smalls_in, 16)
            sp.dma_start(Wt[:, :, :], wt1.rearrange("p (k n) -> p k n", k=KT)).then_inc(wt_in, 16)
            for n in range(G_FOLD):
                if n == 2:
                    sp.dma_start(Wf[:, 0:KT, :], wn1.rearrange("p (m n) -> p m n", m=KT)).then_inc(wn1_in, 16)
                    sp.dma_start(bnb, bn2.partition_broadcast(P)).then_inc(bn2_in, 16)
                if n >= RING:
                    sp.wait_ge(mm_full, n - RING + 1)
                w = w2ta if n < KT else w2to
                sp.dma_start(fold_w[:, n % RING, :, :].rearrange("p k m -> p (k m)"), w[n % KT]).then_inc(fold_in[n % RING], 16)
                if n >= KT + RING:
                    store_fold(sp, n - RING)
            sp.wait_ge(idx_ready, 1)
            sp.dma_start(Wf[:, KT:2 * KT, :], wn2.rearrange("p (k n) -> p k n", k=KT)).then_inc(wn2_in, 16)
            for n in range(G_FOLD - RING, G_FOLD):
                store_fold(sp, n)
            with sp.Fori(0, BLOCKS) as i:
                for j in range(NOTS):
                    for bt in range(RT):
                        g = G0_NOT + j * 2 * KT + KT + 2 * bt + 1
                        sp.wait_ge(act_freed, i * G_NOT + g + 1)
                        sp.dma_start(t_rows[bass.ds(i * BLOCK + (j * B + bt * P), P), :],
                                     t_out[:, bt % 2, :]).then_inc(t_stored[bt % 2], 16)
            for m in range(KT):
                if m < KT // 2:
                    g = G0_NOT + (BLOCKS - 1) * G_NOT + 2 * KT + 2 * m + 1
                else:
                    g = G0_AND - 1
                sp.wait_ge(mm_full, g + 1)
                sp.dma_start(Wf[:, 2 * m:2 * m + 2, :], wa1[m].rearrange("p (s n) -> p s n", s=2)).then_inc(slice_in[m], 16)
            with sp.Fori(0, BLOCKS) as i:
                sp.wait_ge(act_freed, i * G_AND + (G0_AND + G_AND))
                sp.dma_start(and_dram[bass.ds(i * P, P), :],
                             acc[:, :, :].rearrange("p m n -> p (m n)")).then_inc(and_out, 16)
            for m in range(KT):
                sp.wait_ge(mm_full, G0_AND + (BLOCKS - 1) * G_AND + KT + m + 1)
                sp.dma_start(Wf[:, 2 * m:2 * m + 2, :], wo1[m].rearrange("p (s n) -> p s n", s=2)).then_inc(slice_in[m], 16)
            sp.wait_ge(mm_full, G0_OR)
            for s in range(RING):
                sp.wait_ge(fo_out[s], 16 * KT // RING)
            sp.dma_start(Fw[:, :, :], fo_dram.rearrange("p (k n) -> p k n", k=KT)).then_inc(fo_in, 16)
            sp.dma_start(wt2s[:, :, :], wt2.rearrange("p (k n) -> p k n", k=MT1)).then_inc(top_in, 16)
            sp.dma_start(wt1ds[:, :], wt1d).then_inc(top_in, 16)
            sp.wait_ge(and_out, 16 * (1 + BLOCKS))
            with sp.Fori(0, BLOCKS) as i:
                sp.wait_ge(tl_full, i * T_OR + 1)
                sp.dma_start(dens[:, :], dense_t[:, bass.ds(i * BLOCK, BLOCK)]).then_inc(dense_in, 16)
                sp.dma_start(acc[:, :, :].rearrange("p m n -> p (m n)"), and_dram[bass.ds(i * P, P), :]).then_inc(and_in, 16)
                sp.wait_ge(y_ready, i + 1)
                sp.dma_start(out.rearrange("b o -> o b")[:, bass.ds(i * BLOCK, BLOCK)], tmp[0:1, 0, :]).then_inc(y_out, 16)
            sp.wait_ge(y_out, 16 * (1 + BLOCKS))
            for s in range(2):
                sp.wait_ge(t_stored[s], T_STORES)

        @block.gpsimd
        def _(pool):
            def hold(what, value):
                pool.wait_ge(what, value)
                pool.sem_inc(pool_holds, 1)

            def gather(dst, source, bound, index):
                return pool.indirect_dma_start(dst, None, source, bass.IndirectOffsetOnAxis(ap=index, axis=0),
                                               bounds_check=bound, oob_is_err=False)

            def pair_row(tile, slot, buf, n, i=None, per=0):
                gather(rows[:, buf, :], table, ALL_ROWS - 1,
                       stage[:, tile // RT, tile % RT, C_PX + slot:C_PX + slot + 1]).then_inc(x_in[buf], 16)
                hold(x_in[buf], 16 * (n + 1) if i is None else i * per + 16 * (n + 1))
                gather(rows[:, buf, :], t_rows, NOTS * B - 1,
                       stage[:, tile // RT, tile % RT, C_PT + slot:C_PT + slot + 1]).then_inc(row_in[buf], 16)

            hold(idx_ready, 1)
            for t in range(RT):
                gather(not_rows[:, t, :], table, ALL_ROWS - 1, idx[:, t, C_NOT:C_NOT + 1]).then_inc(not_in[t], 16)
            with pool.Fori(0, BLOCKS) as i:
                for t in range(RT):
                    hold(not_in[t], i * 16 + 16)
                pool.tensor_copy(stage[:, 0, :, :], idx[:, bass.ds(i * RT, RT), :]).then_inc(staged, 1)
                pool.tensor_copy(stage[:, 1, :, :], idx[:, bass.ds(i * RT + RT, RT), :]).then_inc(staged, 1)
                hold(staged, i * 2 + 2)
                for j in (1, 0):
                    for t in range(RT):
                        hold(turned[1], i * R_NOT + ((t - RT + 1 if j else t + 1) + R_PRIME))
                        buf = j * RT + t
                        gather(not_rows[:, buf, :], table, ALL_ROWS - 1,
                               stage[:, 1 - j, t, C_NOT + j:C_NOT + j + 1]).then_inc(not_in[buf], 16)

            for s in range(2):
                hold(t_stored[s], T_STORES)
            for t in range(RT):
                hold(not_in[t], 16 * (BLOCKS + 1))
                hold(not_in[RT + t], 16 * BLOCKS)
            pool.tensor_copy(stage[:, 0, :, :], idx[:, 0:RT, :]).then_inc(staged, 1)
            hold(staged, 2 * BLOCKS + 1)
            for n in range(2 * RT):
                if n >= 2:
                    hold(turned[1], R0_AND - 2 * RT + n - 1 + R_PRIME)
                pair_row(n % RT, n // RT, n % 2, n // 2)
            with pool.Fori(0, BLOCKS) as i:
                for s in range(2):
                    hold(row_in[s], i * (16 * R_AND // 2) + 16 * RT)
                pool.tensor_copy(stage[:, 0, :, :], idx[:, bass.ds(i * RT, RT), :]).then_inc(staged, 1)
                pool.tensor_copy(stage[:, 1, :, :], idx[:, bass.ds(i * RT + RT, RT), :]).then_inc(staged, 1)
                hold(staged, i * 2 + (2 * BLOCKS + 3))
                for n in range(R_AND):
                    hold(turned[1], i * R_AND + (R0_AND + n - 1 + R_PRIME))
                    pair = 1 - n // (2 * RT)
                    pair_row((1 - pair) * RT + n % RT, 2 * pair + n // RT % 2, n % 2,
                             RT + n // 2, i, 16 * R_AND // 2)
            used = RT + BLOCKS * R_AND // 2
            for s in range(2):
                hold(row_in[s], 16 * used)
            pool.tensor_copy(stage[:, 0, :, :], idx[:, 0:RT, :]).then_inc(staged, 1)
            hold(staged, 4 * BLOCKS + 2)
            for n in range(2 * RT):
                hold(turned[1], R0_OR - 2 * RT + n - 1 + R_PRIME)
                pair_row(n % RT, 2 * AND_PAIRS + n // RT, n % 2, used + n // 2)
            with pool.Fori(0, BLOCKS) as i:
                for s in range(2):
                    hold(row_in[s], i * (16 * RT) + 16 * (used + RT))
                hold(rem_added, i * (REM * RT) + 1)
                pool.tensor_copy(stage[:, 0, :, :], idx[:, bass.ds(i * RT, RT), :]).then_inc(staged, 1)
                pool.tensor_copy(stage[:, 1, :, :], idx[:, bass.ds(i * RT + RT, RT), :]).then_inc(staged, 1)
                hold(staged, i * 2 + (4 * BLOCKS + 4))
                for n in range(REM * RT):
                    t, c = n // REM, n % REM
                    if n >= 3:
                        hold(rem_added, i * (REM * RT) + (n - 1))
                    pool.memset(rem_in[:, n % 3, :], 0.0).then_inc(zeroed, 1)
                    hold(zeroed, i * (REM * RT) + (n + 1))
                    source, bound = (table, ALL_ROWS - 1) if c < F else (t_rows, NOTS * B - 1)
                    gather(rem_in[:, n % 3, :], source, bound, stage[:, 0, t, C_RX + c:C_RX + c + 1]).then_inc(rem_got[n % 3], 16)
                for n in range(2 * RT):
                    hold(turned[1], i * R_OR + (R0_OR + (RT if n > 1 else 0) + n - 1 + R_PRIME))
                    pair_row(RT + n % RT, 2 * AND_PAIRS + n // RT, n % 2, used + RT + n // 2, i, 16 * RT)

        @block.tensor
        def _(pe):
            pe.sem_inc(turned[1], R_PRIME)
            pe.wait_ge(consts_in, 16)
            pe.wait_ge(wt_in, 16)

            def turn(src, r, i=None, per=0):
                for h in range(2):
                    pe.wait_ge(taken[h], r if i is None else i * per + r)
                    for k in range(KT // 2):
                        kk = h * (KT // 2) + k
                        last = pe.transpose(tp[:, h, k * P:(k + 1) * P], src[:, kk * P:(kk + 1) * P], ident)
                    last.then_inc(turned[h], 1)

            for n in range(G_FOLD):
                pe.wait_ge(fold_in[n % RING], 16 * (n // RING + 1))
                if n >= RING:
                    pe.wait_ge(act_freed, n - RING + 1)
                for k in range(KT):
                    last = pe.matmul(mm[:, n % RING, :], fold_w[:, n % RING, k, :], Wt[:, k, :],
                                     start=(k == 0), stop=(k == KT - 1))
                last.then_inc(mm_full, 1)
            pe.wait_ge(bvec_ready, 1)
            for m in range(MT1):
                for k in range(KT):
                    last = pe.matmul(tl[:, 0, m:m + 1], Wt[:, k, m * P:(m + 1) * P], bvec[:, k:k + 1],
                                     start=(k == 0), stop=(k == KT - 1))
            last.then_inc(tl_full, 1)

            for t in range(RT):
                pe.wait_ge(not_in[t], 16)
                turn(not_rows[:, t, :], t)
            pe.wait_ge(wn1_in, 16)
            pe.wait_ge(wn2_in, 16)
            with pe.Fori(0, BLOCKS) as i:
                for j in range(NOTS):
                    r_have = R0_NOT + j * RT
                    for h in range(2):
                        pe.wait_ge(taken[h], i * R_NOT + r_have)
                    for m in range(KT):
                        g = G0_NOT + j * 2 * KT + m
                        pe.wait_ge(act_freed, i * G_NOT + (g - RING + 1))
                        for k in range(KT):
                            last = pe.matmul(mm[:, g % RING, :], Wf[:, m, k * P:(k + 1) * P], X[:, j, k, :],
                                             start=(k == 0), stop=(k == KT - 1))
                        last.then_inc(mm_full, 1)
                    for bt in range(RT):
                        buf = (1 - j) * RT + bt
                        pe.wait_ge(not_in[buf], i * 16 + (16 if j == 0 else 32))
                        turn(not_rows[:, buf, :], R0_NOT + j * RT + bt, i, R_NOT)
                        if bt == 0:
                            pe.wait_ge(act_freed, i * G_NOT + (G0_NOT + j * 2 * KT + KT))
                        for nh in range(2):
                            g = G0_NOT + j * 2 * KT + KT + 2 * bt + nh
                            pe.wait_ge(act_freed, i * G_NOT + (g - RING + 1))
                            for k in range(KT):
                                last = pe.matmul(mm[:, g % RING, :], Hb[:, k, bt * P:(bt + 1) * P],
                                                 Wf[:, KT + k, nh * HALF:(nh + 1) * HALF],
                                                 start=(k == 0), stop=(k == KT - 1))
                            last.then_inc(mm_full, 1)

            def pair_layer(g0, per, i, r, s0, slice_count, between):
                for h in range(2):
                    pe.wait_ge(taken[h], r)
                for m in range(KT):
                    pe.wait_ge(slice_in[m], slice_count)
                    ring_wait(g0 + m, per, i)
                    for k in range(2 * KT):
                        w = Wf[:, 2 * m + k // KT, (k % KT) * P:(k % KT + 1) * P]
                        last = pe.matmul(mm[:, (g0 + m) % RING, :], w, X[:, s0 + k // KT, k % KT, :],
                                         start=(k == 0), stop=(k == 2 * KT - 1))
                    last.then_inc(mm_full, 1)
                    between(m)

            def ring_wait(g, per, i):
                pe.wait_ge(act_freed, i * per + (g - RING + 1))

            for n in range(2 * RT):
                pe.wait_ge(row_in[n % 2], 16 * (n // 2 + 1))
                turn(rows[:, n % 2, :], R0_AND - 2 * RT + n)
            with pe.Fori(0, BLOCKS) as i:
                for pair in range(AND_PAIRS):
                    def between(m):
                        n = pair * 2 * RT + m
                        pe.wait_ge(row_in[n % 2], i * (16 * R_AND // 2) + 16 * (RT + n // 2 + 1))
                        turn(rows[:, n % 2, :], R0_AND + n, i, R_AND)
                    pair_layer(G0_AND + pair * KT, G_AND, i, i * R_AND + (R0_AND + pair * 2 * RT),
                               2 * pair, 16, between)
                pe.wait_ge(summed, i * KT + (KT + 1))
                for m in range(MT1):
                    g = G0_AND + AND_PAIRS * KT + m
                    ring_wait(g, G_AND, i)
                    for k in range(KT):
                        last = pe.matmul(mm[:, g % RING, :], Fw[:, k, m * P:(m + 1) * P], Hb[:, k, :],
                                         start=(k == 0), stop=(k == KT - 1))
                    last.then_inc(mm_full, 1)

            used = RT + BLOCKS * R_AND // 2
            for n in range(2 * RT):
                pe.wait_ge(row_in[n % 2], 16 * (used + n // 2 + 1))
                turn(rows[:, n % 2, :], R0_OR - 2 * RT + n)
            pe.wait_ge(act_freed, G0_OR)
            pe.wait_ge(fo_in, 16)
            pe.wait_ge(top_in, 32)
            with pe.Fori(0, BLOCKS) as i:
                for h in range(2):
                    pe.wait_ge(taken[h], i * R_OR + R0_OR)
                for m in range(KT):
                    pe.wait_ge(slice_in[m], 32)
                    if m < RING:
                        pe.wait_ge(dve_freed, i * MT1 + m + 1)
                    else:
                        pe.wait_ge(act_freed, i * KT + (G0_OR + m - RING + 1))
                    for k in range(2 * KT):
                        w = Wf[:, 2 * m + k // KT, (k % KT) * P:(k % KT + 1) * P]
                        last = pe.matmul(mm[:, m % RING, :], w, X[:, k // KT, k % KT, :],
                                         start=(k == 0), stop=(k == 2 * KT - 1))
                    last.then_inc(mm_full, 1)
                    if m % 2:
                        pe.wait_ge(rem_summed, i * RT + (m // 2 + 1))
                        turn(rem_sum, R0_OR + m // 2, i, R_OR)
                pe.wait_ge(act_freed, i * KT + (G0_OR + KT))
                for h in range(2):
                    pe.wait_ge(taken[h], i * R_OR + (R0_OR + RT))
                pe.wait_ge(dense_in, i * 16 + 16)
                for m in range(MT1):
                    for k in range(2 * KT):
                        w = (Fw if k < KT else Wt)[:, k % KT, m * P:(m + 1) * P]
                        x = Hb[:, k % KT, :] if k < KT else X[:, 2, k % KT, :]
                        last = pe.matmul(mm[:, m % RING, :], w, x, start=(k == 0), stop=(k == 2 * KT - 1))
                    last.then_inc(mm_full, 1)
                    pe.wait_ge(tl_freed, i * T_OR + max(m, 1))
                    pe.matmul(tl[:, m % 2, :], wt1ds[:, m * P:(m + 1) * P], dens[:, :],
                              start=True, stop=True).then_inc(tl_full, 1)
                    for n in (2 * m, 2 * m + 1):
                        pe.wait_ge(row_in[n % 2], i * (16 * RT) + 16 * (used + RT + n // 2 + 1))
                        turn(rows[:, n % 2, :], R0_OR + RT + n, i, R_OR)
                pe.wait_ge(h1_ready, i * MT1 + MT1)
                for m in range(MT2):
                    pe.wait_ge(tl_freed, i * T_OR + (MT1 + m))
                    for k in range(MT1):
                        last = pe.matmul(tl[:, m % 2, :], wt2s[:, k, m * P:(m + 1) * P], acc[:, k, :],
                                         start=(k == 0), stop=(k == MT1 - 1))
                    last.then_inc(tl_full, 1)
                pe.wait_ge(tl_freed, i * T_OR + (MT1 + MT2 + 1))
                for k in range(MT2):
                    last = pe.matmul(tl[0:1, 0, :], small[:, S_W3 + k:S_W3 + k + 1], Hb[:, k, :],
                                     start=(k == 0), stop=(k == MT2 - 1))
                last.then_inc(tl_full, 1)

        @block.scalar
        def _(act):
            def take(r, slot, t, i=None, per=0):
                act.wait_ge(turned[1], (r if i is None else i * per + r) + (1 + R_PRIME))
                nc.scalar.activation(X[:, slot, KT // 2:KT, t * P:(t + 1) * P],
                                     tp[:, 1, :].rearrange("p (k b) -> p k b", k=KT // 2),
                                     ACT.Copy).then_inc(taken[1], 1)

            for n in range(G_FOLD):
                act.wait_ge(mm_full, n + 1)
                if n < KT:
                    dst = Fw[:, n, :]
                else:
                    dst = acc[:, n % RING, :]
                    if n >= KT + RING:
                        act.wait_ge(fo_out[n % RING], 16 * ((n - KT) // RING))
                nc.scalar.activation(dst, mm[:, n % RING, :], ACT.Copy).then_inc(act_freed, 1)
            for s in range(RING):
                act.wait_ge(fo_out[s], 16 * KT // RING)
            act.wait_ge(smalls_in, 16)
            for t in range(RT):
                take(t, 0, t)
            with act.Fori(0, BLOCKS) as i:
                for j in range(NOTS):
                    for m in range(KT):
                        g = G0_NOT + j * 2 * KT + m
                        act.wait_ge(mm_full, i * G_NOT + (g + 1))
                        nc.scalar.activation(Hb[:, m, :], mm[:, g % RING, :], ACT.Relu,
                                             bias=small[:, S_N1 + m:S_N1 + m + 1]).then_inc(act_freed, 1)
                    for bt in range(RT):
                        take(R0_NOT + j * RT + bt, 1 - j, bt, i, R_NOT)
                        act.wait_ge(t_stored[bt % 2], i * (16 * NOTS * RT // 2) + 16 * (1 + j * RT // 2 + bt // 2))
                        for nh in range(2):
                            g = G0_NOT + j * 2 * KT + KT + 2 * bt + nh
                            act.wait_ge(biased, i * (NOTS * KT) + (j * KT + 2 * bt + nh + 1))
                            nc.scalar.activation(t_out[:, bt % 2, nh * HALF:(nh + 1) * HALF],
                                                 mm[:, g % RING, :], ACT.Tanh).then_inc(act_freed, 1)
            for s in range(2):
                act.wait_ge(t_stored[s], T_STORES)
            for n in range(2 * RT):
                take(R0_AND - 2 * RT + n, n // RT, n % RT)
            with act.Fori(0, BLOCKS) as i:
                for pair in range(AND_PAIRS):
                    for m in range(KT):
                        g = G0_AND + pair * KT + m
                        act.wait_ge(mm_full, i * G_AND + (g + 1))
                        if pair:
                            act.wait_ge(summed, i * KT + max(m, 1))
                        dst = tmp[:, m % 2, :] if pair else Hb[:, m, :]
                        nc.scalar.activation(dst, mm[:, g % RING, :], ACT.Relu,
                                             bias=small[:, S_A1 + m:S_A1 + m + 1]).then_inc(act_freed, 1)
                        n = pair * 2 * RT + m
                        take(R0_AND + n, 2 * (1 - pair) + m // RT, m % RT, i, R_AND)
                act.wait_ge(and_out, i * 16 + 16)
                for m in range(MT1):
                    g = G0_AND + AND_PAIRS * KT + m
                    act.wait_ge(mm_full, i * G_AND + (g + 1))
                    nc.scalar.activation(acc[:, m, :], mm[:, g % RING, :], ACT.Copy).then_inc(act_freed, 1)
            for n in range(2 * RT):
                take(R0_OR - 2 * RT + n, n // RT, n % RT)
            with act.Fori(0, BLOCKS) as i:
                for m in range(KT):
                    act.wait_ge(mm_full, i * G_OR + (G0_OR + m + 1))
                    nc.scalar.activation(Hb[:, m, :], mm[:, m % RING, :], ACT.Relu,
                                         bias=small[:, S_O1 + m:S_O1 + m + 1]).then_inc(act_freed, 1)
                    if m % 2:
                        take(R0_OR + m // 2, 2, m // 2, i, R_OR)
                for m in range(MT1):
                    for n in (2 * m, 2 * m + 1):
                        take(R0_OR + RT + n, n // RT, n % RT, i, R_OR)
                    act.wait_ge(acc_step, i * (2 * MT1) + (2 * m + 2))
                    nc.scalar.activation(acc[:, m, :], acc[:, m, :], ACT.Relu,
                                         bias=c1[:, m:m + 1]).then_inc(h1_ready, 1)
                for m in range(MT2):
                    act.wait_ge(tl_full, i * T_OR + (1 + MT1 + m + 1))
                    nc.scalar.activation(Hb[:, m, :], tl[:, m % 2, :], ACT.Relu,
                                         bias=small[:, S_T2 + m:S_T2 + m + 1]).then_inc(tl_freed, 1)
                act.wait_ge(tl_full, i * T_OR + (1 + T_OR))
                act.wait_ge(y_out, i * 16 + 16)
                nc.scalar.activation(tmp[0:1, 0, :], tl[0:1, 0, :], ACT.Copy).then_inc(y_ready, 1)
                act.wait_ge(y_ready, i + 1)
                act.sem_inc(tl_freed, 1)

        @block.vector
        def _(dve):
            steps = [0]

            def step(ins):
                steps[0] += 1
                ins.then_inc(setup, 1)
                dve.wait_ge(setup, steps[0])

            dve.sem_inc(dve_freed, RING)
            dve.sem_inc(tl_freed, 1)
            dve.sem_inc(rem_added, 1)
            dve.sem_inc(summed, 1)
            V = nc.vector
            dve.wait_ge(consts_in, 16)
            dve.wait_ge(ints_in, 32)
            at = [TILES * F + F]

            def scratch(*shape):
                n = int(np.prod(shape))
                v = scr_f[:, at[0]:at[0] + n]
                at[0] += n
                if len(shape) == 2:
                    v = v.rearrange("p (a b) -> p a b", a=shape[0])
                return v

            scr_f = W[:, 13:16, :].rearrange("p s n -> p (s n)")
            at[0] = 0
            ids_i = scr[:, 0:TILES * F].bitcast(i32).rearrange("p (t f) -> p t f", f=F)
            fields_i = scr[:, TILES * F:TILES * F + F].bitcast(i32)
            Q = NOTS + SLOTS
            which = scratch(Q)
            neg8 = scratch(Q)
            loc, wrap = scratch(TILES, F), scratch(TILES, F)
            eq = scratch(Q, F)
            prod = scratch(TILES, F)
            row = scratch(TILES, Q)
            notf, used, rest, valid = scratch(F), scratch(F), scratch(F), scratch(F)
            e6 = scratch(SLOTS, F)
            isn, in0, keep, trow = scratch(SLOTS), scratch(SLOTS), scratch(SLOTS), scratch(SLOTS)
            vt, cnt, e2 = scratch(NOTS), scratch(1), scratch(NOTS, F)
            idxf = scratch(TILES, COLS)
            field_no, start, last_id = (cst[:, k:k + F] for k in (K_FIELD, K_START, K_LAST))
            batch_no = cst[:, K_ROW:K_ROW + TILES]

            def over_tiles(v, n):
                return v.unsqueeze(1).to_broadcast([P, TILES, n])

            step(V.tensor_copy(which, fields_i))
            step(V.tensor_scalar(neg8, which, 0.0, float(F), ALU.is_lt, ALU.mult))
            step(V.tensor_tensor(which, which, neg8, ALU.add))
            step(V.tensor_copy(loc, ids_i))
            step(V.tensor_scalar(wrap, loc, 0.0, None, ALU.is_lt))
            step(V.tensor_tensor(prod, wrap, over_tiles(last_id, F), ALU.mult))
            step(V.tensor_tensor(loc, loc, prod, ALU.add))
            step(V.tensor_tensor(loc, loc, wrap, ALU.add))
            step(V.tensor_scalar(loc, loc, 0.0, None, ALU.max))
            step(V.tensor_tensor(loc, loc, over_tiles(last_id, F), ALU.min))
            step(V.tensor_tensor(loc, loc, over_tiles(start, F), ALU.add))
            step(V.tensor_tensor(eq, field_no.unsqueeze(1).to_broadcast([P, Q, F]),
                                 which.unsqueeze(2).to_broadcast([P, Q, F]), ALU.is_equal))
            for q in range(Q):
                step(V.tensor_tensor(prod, loc, over_tiles(eq[:, q, :], F), ALU.mult))
                step(V.tensor_reduce(row[:, :, q:q + 1], prod, AX.X, ALU.add))
            step(V.tensor_tensor(notf, eq[:, 0, :], eq[:, 1, :], ALU.max))
            pairs = eq[:, NOTS:Q, :]
            step(V.tensor_tensor(e6, pairs, notf.unsqueeze(1).to_broadcast([P, SLOTS, F]), ALU.mult))
            step(V.tensor_reduce(isn, e6, AX.X, ALU.add))
            step(V.tensor_tensor(e6, pairs, eq[:, 0, :].unsqueeze(1).to_broadcast([P, SLOTS, F]), ALU.mult))
            step(V.tensor_reduce(in0, e6, AX.X, ALU.add))
            step(V.tensor_reduce(used, pairs.rearrange("p q f -> p f q"), AX.X, ALU.max))
            step(V.tensor_scalar(rest, used, -1.0, 1.0, ALU.mult, ALU.add))
            step(V.tensor_reduce(cnt, rest, AX.X, ALU.add))
            step(V.tensor_scalar(cnt, cnt, float(AND_PAIRS + OR_PAIRS), None, ALU.add))
            step(V.reciprocal(invc[:, :], cnt))
            step(V.tensor_copy(idxf[:, :, C_NOT:C_NOT + NOTS], row[:, :, 0:NOTS]))

            def masked(cols, n, rows_ap, mask):
                dst = idxf[:, :, cols:cols + n]
                step(V.tensor_scalar(dst, rows_ap, -float(SKIP), None, ALU.add))
                step(V.tensor_tensor(dst, dst, over_tiles(mask, n), ALU.mult))
                step(V.tensor_scalar(dst, dst, float(SKIP), None, ALU.add))

            step(V.tensor_scalar(keep, isn, -1.0, 1.0, ALU.mult, ALU.add))
            masked(C_PX, SLOTS, row[:, :, NOTS:Q], keep)
            step(V.tensor_scalar(trow, in0, -float(B), float(B), ALU.mult, ALU.add))
            tr = idxf[:, :, C_PT:C_PT + SLOTS]
            step(V.tensor_tensor(tr, batch_no.unsqueeze(2).to_broadcast([P, TILES, SLOTS]),
                                 over_tiles(trow, SLOTS), ALU.add))
            masked(C_PT, SLOTS, tr, isn)
            step(V.tensor_scalar(valid, notf, -1.0, 1.0, ALU.mult, ALU.add))
            step(V.tensor_tensor(valid, valid, rest, ALU.mult))
            masked(C_RX, F, loc, valid)
            step(V.tensor_tensor(e2[:, 0, :], rest, eq[:, 0, :], ALU.mult))
            step(V.tensor_tensor(e2[:, 1, :], rest, eq[:, 1, :], ALU.mult))
            step(V.tensor_scalar(valid, eq[:, 0, :], -1.0, 1.0, ALU.mult, ALU.add))
            step(V.tensor_tensor(e2[:, 1, :], e2[:, 1, :], valid, ALU.mult))
            step(V.tensor_reduce(vt, e2, AX.X, ALU.add))
            for j in range(NOTS):
                step(V.tensor_scalar(idxf[:, :, C_RT + j], batch_no, float(j * B), None, ALU.add))
            masked(C_RT, NOTS, idxf[:, :, C_RT:C_RT + NOTS], vt)
            step(V.tensor_copy(idx[:, 0:TILES, :], idxf))
            V.tensor_copy(idx[:, TILES:TILES + RT, :], idxf[:, 0:RT, :]).then_inc(idx_ready, 1)

            dve.wait_ge(smalls_in, 16)
            step(V.tensor_scalar(bvec[:, :], small[:, S_A2:S_A2 + KT], float(AND_PAIRS), None, ALU.mult))
            V.scalar_tensor_tensor(out=bvec[:, :], in0=small[:, S_O2:S_O2 + KT], scalar=float(OR_PAIRS),
                                   in1=bvec[:, :], op0=ALU.mult, op1=ALU.add).then_inc(bvec_ready, 1)
            dve.wait_ge(tl_full, 1)
            V.scalar_tensor_tensor(out=c1[:, :], in0=tl[:, 0, 0:MT1], scalar=invc[:, 0:1],
                                   in1=small[:, S_T1:S_T1 + MT1], op0=ALU.mult, op1=ALU.add).then_inc(c1_ready, 1)

            def take(r, slot, t, i=None, per=0):
                dve.wait_ge(turned[0], (r if i is None else i * per + r) + 1)
                V.tensor_copy(X[:, slot, 0:KT // 2, t * P:(t + 1) * P],
                              tp[:, 0, :].rearrange("p (k b) -> p k b", k=KT // 2)).then_inc(taken[0], 1)

            for t in range(RT):
                take(t, 0, t)
            dve.wait_ge(bn2_in, 16)
            with dve.Fori(0, BLOCKS) as i:
                for j in range(NOTS):
                    for bt in range(RT):
                        take(R0_NOT + j * RT + bt, 1 - j, bt, i, R_NOT)
                        for nh in range(2):
                            g = G0_NOT + j * 2 * KT + KT + 2 * bt + nh
                            dve.wait_ge(mm_full, i * G_NOT + (g + 1))
                            V.tensor_tensor(mm[:, g % RING, :], mm[:, g % RING, :],
                                            bnb[:, nh * HALF:(nh + 1) * HALF], ALU.add).then_inc(biased, 1)
            for n in range(2 * RT):
                take(R0_AND - 2 * RT + n, n // RT, n % RT)
            with dve.Fori(0, BLOCKS) as i:
                for pair in range(AND_PAIRS):
                    for m in range(KT):
                        if pair:
                            g = G0_AND + pair * KT + m
                            dve.wait_ge(act_freed, i * G_AND + (g + 1))
                            V.tensor_tensor(Hb[:, m, :], Hb[:, m, :], tmp[:, m % 2, :], ALU.add).then_inc(summed, 1)
                        take(R0_AND + pair * 2 * RT + m, 2 * (1 - pair) + m // RT, m % RT, i, R_AND)
            for n in range(2 * RT):
                take(R0_OR - 2 * RT + n, n // RT, n % RT)
            dve.wait_ge(c1_ready, 1)
            with dve.Fori(0, BLOCKS) as i:
                for t in range(RT):
                    for c in range(REM):
                        n = t * REM + c
                        n_s = len(range(n % 3, REM * RT, 3))
                        dve.wait_ge(rem_got[n % 3], i * (16 * n_s) + 16 * (n // 3 + 1))
                        if c == 0:
                            dve.wait_ge(turned[1], i * R_OR + (R0_OR - 2 * RT if t == 0 else R0_OR + t) + R_PRIME)
                            ins = V.tensor_copy(rem_sum, rem_in[:, n % 3, :])
                        else:
                            dve.wait_ge(rem_added, i * (REM * RT) + (n + 1))
                            ins = V.tensor_tensor(rem_sum, rem_sum, rem_in[:, n % 3, :], ALU.add)
                        ins.then_inc(rem_added, 1)
                    dve.wait_ge(rem_added, i * (REM * RT) + ((t + 1) * REM + 1))
                    dve.sem_inc(rem_summed, 1)
                    take(R0_OR + t, 2, t, i, R_OR)
                dve.wait_ge(and_in, i * 16 + 16)
                for m in range(MT1):
                    dve.wait_ge(mm_full, i * G_OR + (G0_OR + KT + m + 1))
                    V.tensor_tensor(acc[:, m, :], mm[:, m % RING, :], acc[:, m, :], ALU.add).then_inc(acc_step, 1)
                    dve.wait_ge(acc_step, i * (2 * MT1) + (2 * m + 1))
                    dve.sem_inc(dve_freed, 1)
                    dve.wait_ge(tl_full, i * T_OR + (1 + m + 1))
                    V.scalar_tensor_tensor(out=acc[:, m, :], in0=acc[:, m, :], scalar=invc[:, 0:1],
                                           in1=tl[:, m % 2, :], op0=ALU.mult, op1=ALU.add).then_inc(acc_step, 1)
                    dve.wait_ge(acc_step, i * (2 * MT1) + (2 * m + 2))
                    dve.sem_inc(tl_freed, 1)
                    for n in (2 * m, 2 * m + 1):
                        take(R0_OR + RT + n, n // RT, n % RT, i, R_OR)


def weight_slices(w):
    k, m = w.shape
    return np.ascontiguousarray(w.reshape(k // P, P, m // P, P).transpose(2, 1, 0, 3)).reshape(m // P, P, k)


def by_partition(w):
    k, n = w.shape
    return np.ascontiguousarray(w.reshape(k // P, P, n).transpose(1, 0, 2)).reshape(P, k // P * n)


def kernel(**inputs):
    import concourse.bacc as bacc
    from concourse.bass_utils import run_bass_kernel_spmd

    a = {k: np.asarray(v) for k, v in inputs.items()}
    consts = np.zeros((P, K_COLS), np.float32)
    consts[:, K_FIELD:K_FIELD + F] = np.arange(F)
    consts[:, K_START:K_START + F] = TABLE_START
    consts[:, K_LAST:K_LAST + F] = [n - 1 for n in TABLE_ROWS]
    consts[:, K_ROW:K_ROW + TILES] = np.arange(B).reshape(TILES, P).T
    consts[:, K_IDENT:] = np.eye(P)
    w_top1, w_z = a["W_top1"], a["W_top1"][:H]
    names = ["L0_rec_bn1", "L0_rec_ba1", "L0_rec_bo1", "L0_rec_ba2", "L0_rec_bo2", "b_top1", "b_top2"]
    smalls = [a[n].reshape(-1, P).T for n in names] + [a["W_top3"].reshape(MT2, P).T]
    n1 = weight_slices(a["L0_rec_Wn1"])
    data = {
        "table": np.concatenate([a[f"tbl_{f}"] for f in range(F)], axis=0),
        "ids": np.ascontiguousarray(a["ids"].reshape(TILES, P, F).transpose(1, 0, 2)).reshape(P, TILES * F),
        "fields": np.concatenate([a["L0_rec_not_idx"].reshape(-1), a["L0_rec_and_pairs"].reshape(-1),
                                  a["L0_rec_or_pairs"].reshape(-1)]),
        "consts": consts,
        "smalls": np.ascontiguousarray(np.concatenate(smalls, axis=1)),
        "bn2": a["L0_rec_bn2"],
        "wn1": np.ascontiguousarray(n1.transpose(1, 0, 2)).reshape(P, KT * H),
        "wn2": by_partition(a["L0_rec_Wn2"]),
        "wa1": weight_slices(a["L0_rec_Wa1"]),
        "wo1": weight_slices(a["L0_rec_Wo1"]),
        "w2ta": weight_slices(a["L0_rec_Wa2"].T),
        "w2to": weight_slices(a["L0_rec_Wo2"].T),
        "wt1": by_partition(w_z),
        "wt1d": np.ascontiguousarray(w_top1[H:]),
        "wt2": by_partition(a["W_top2"]),
        "dense_t": np.ascontiguousarray(a["dense_ctx"].T),
    }
    nc = bacc.Bacc("TRN2", target_bir_lowering=False, num_devices=1)
    args = {k: nc.dram_tensor(f"in_{k}", v.shape, mybir.dt.from_np(v.dtype), kind="ExternalInput").ap()
            for k, v in data.items()}
    y = nc.dram_tensor("y", (B, 1), mybir.dt.float32, kind="ExternalOutput").ap()
    build(nc, **args, out=y)
    r = run_bass_kernel_spmd(nc, [{f"in_{k}": v for k, v in data.items()}], core_ids=[0])
    return r.results[0]["y"]
```

```python
from contextlib import ExitStack

import numpy as np

import concourse.bass as bass
from concourse import mybir

B, F, H = 2048, 8, 1024
D, M1, M2 = 16, 512, 256
TABLE_ROWS = [1250, 1000, 1250, 12500, 1000, 1250, 12500, 1250]
TABLE_START = [sum(TABLE_ROWS[:f]) for f in range(F)]
ALL_ROWS = sum(TABLE_ROWS)
NOTS, AND_PAIRS, OR_PAIRS = 2, 2, 1
P = 128
KT = H // P
MT1, MT2 = M1 // P, M2 // P
BLOCK = 512
BLOCKS = B // BLOCK
RT = BLOCK // P
TILES = B // P
HALF = H // 2

SLOTS = 2 * (AND_PAIRS + OR_PAIRS)
C_NOT = 0
C_PX = C_NOT + NOTS
C_PT = C_PX + SLOTS
C_ALL = C_PT + SLOTS
COLS = C_ALL + F
SKIP = 1 << 20

K_FIELD, K_START, K_LAST, K_ROW, K_IDENT = 0, F, 2 * F, 3 * F, 3 * F + TILES
K_COLS = K_IDENT + P
S_N1, S_A1, S_O1, S_A2, S_O2 = 0, KT, 2 * KT, 3 * KT, 4 * KT
S_T1 = 5 * KT
S_T2 = S_T1 + MT1
S_W3 = S_T2 + MT2
S_COLS = S_W3 + MT2

RING = 4
G_FOLD = 2 * KT
G_NOT = NOTS * 2 * KT
G_AND = AND_PAIRS * KT + MT1
G_OR = KT + 2 * MT1
G0_NOT = G_FOLD
G0_AND = G0_NOT + BLOCKS * G_NOT
G0_OR = G0_AND + BLOCKS * G_AND
R_NOT, R_AND, R_OR = NOTS * RT, 2 * AND_PAIRS * RT, 3 * RT
R0_NOT = RT
R0_AND = R0_NOT + BLOCKS * R_NOT + 2 * RT
R0_OR = R0_AND + BLOCKS * R_AND + 2 * RT
T_OR = MT1 + MT2 + 1
T_STORES = 16 * (1 + BLOCKS * NOTS * RT // 2)
R_STORES = 16 * (1 + BLOCKS * RT // 2)
SEEN = F * RT
SPLIT_NOT = 1 + BLOCKS * NOTS * KT
SPLIT_AND = SPLIT_NOT + BLOCKS * AND_PAIRS * KT
PAIR_SLICES, SLICE = 2 * KT, 2 * H
IN_N2, IN_FA, IN_FO, IN_WT = KT, 2 * KT, 2 * KT + KT // 2, 3 * KT
X_BN1, X_BA1, X_BO1, X_N1, X_N2, X_FA, X_FO, X_WT, X_ROW, X_JOB, X_ALL = 0, 1, 2, 3, 4, 5, 6, 7, 8, 10, 12
U_N1, U_N2, U_FA, U_FO, U_WT, U_X, U_H, U_ALL, U_RA, U_RO, U_REM, U_JOB = 0, 1, 2, 3, 4, 5, 7, 9, 10, 11, 12, 13
V_NOT1, V_NOT2, V_TOPA, V_TOPO, V_TOPR, V_BOUND = 0, 2, 4, 5, 6, 7
EXPONENT = 0x7F800000
LEAST = 2.0 ** -46
NOT_STEPS = NOTS * 34


def build(nc, table, ids, fields, consts, smalls, bn2, wn1, wn2, pair_w, w2ta, w2to, wt1, wt1d,
          wt2, dense_t, out):
    fp32, fp16, i32 = mybir.dt.float32, mybir.dt.float16, mybir.dt.int32
    ALU, ACT, AX = mybir.AluOpType, mybir.ActivationFunctionType, mybir.AxisListType
    MAX = bass.bass_isa.ReduceOp.max

    ctx = ExitStack()
    with ctx:
        def sb(name, shape, dt=fp32):
            return ctx.enter_context(nc.sbuf_tensor(name, shape, dt))

        def sem(name):
            return ctx.enter_context(nc.semaphore(name))

        def dram(name, shape, dt=fp32):
            return nc.dram_tensor(name, shape, dt, kind="Internal").ap()

        t_rows = dram("t_rows", (NOTS * B, H))
        and_dram = dram("and_dram", (BLOCKS * P, MT1 * BLOCK))
        pair_split = dram("pair_split", (PAIR_SLICES, P, 2 * SLICE), fp16)
        fo_split = dram("fo_split", (P, 2 * KT * M1), fp16)
        wt_split = dram("wt_split", (P, 2 * KT * M1), fp16)
        rem_rows = dram("rem_rows", (B, H))
        token = dram("token", (7, P))

        W = sb("W", [P, 16 * 2 * H], fp16)
        X = sb("X", [P, 4, 2, KT, BLOCK], fp16)
        Hb = sb("Hb", [P, 2, KT, BLOCK], fp16)
        Fw = sb("Fw", [P, 2 * KT * M1], fp16)
        Wt = sb("Wt", [P, 2 * KT * M1], fp16)
        rows = sb("rows", [P, 2, H])
        acc = sb("acc", [P, MT1, BLOCK])
        tmp = sb("tmp", [P, 2, BLOCK])
        side = sb("side", [P, 2, BLOCK])
        cst = sb("cst", [P, K_COLS])
        small = sb("small", [P, S_COLS])
        bvec = sb("bvec", [P, KT])
        c1 = sb("c1", [P, MT1])
        invc = sb("invc", [P, 1])
        rem_w = sb("rem_w", [P, F + NOTS])
        idx = sb("idx", [P, TILES + RT, COLS], i32)
        stage = sb("stage", [P, 2, RT, COLS], i32)
        part_max = sb("part_max", [P, 16])
        all_max = sb("all_max", [P, 16])
        piece = sb("piece", [P, 16])
        up = sb("up", [P, 16])
        down = sb("down", [P, 16])
        u = sb("u", [P, 16])
        rowmax = sb("rowmax", [P, 8])
        slice_max = sb("slice_max", [P, PAIR_SLICES])
        slice_down = sb("slice_down", [P, PAIR_SLICES])
        u_pair = sb("u_pair", [P, PAIR_SLICES])
        b_not = sb("b_not", [P, NOTS, KT])
        b_pair = sb("b_pair", [P, 2, KT])
        field_run = sb("field_run", [P, 2])

        ident = cst[:, K_IDENT:K_IDENT + P]
        W_not = W[:, :].rearrange("p (s h n) -> p s h n", s=16, h=2)
        W_pair = W[:, :].rearrange("p (s h n) -> p s h n", s=KT, h=2)
        Fs = Fw[:, :].rearrange("p (s h n) -> p s h n", s=KT // 2, h=2)
        Ts = Wt[:, :].rearrange("p (s h n) -> p s h n", s=KT // 2, h=2)
        F32 = Fw[:, :].bitcast(fp32).rearrange("p (k n) -> p k n", k=KT)
        T32 = Wt[:, :].bitcast(fp32).rearrange("p (k n) -> p k n", k=KT)

        def as_rows(slot):
            return X[:, slot, :, :, :].rearrange("p h k n -> p (h k n)").bitcast(fp32)

        scr = as_rows(0)
        fold_w = as_rows(1).rearrange("p (s k m) -> p s k m", s=RING, k=KT)
        not_rows = as_rows(2).rearrange("p (s n) -> p s n", n=H)
        job_in_f = as_rows(3)[:, 0:SLICE]
        job_out = as_rows(3)[:, SLICE:2 * SLICE].bitcast(fp16).rearrange("p (h n) -> p h n", h=2)
        Fo32 = as_rows(3).rearrange("p (k n) -> p k n", k=KT)
        Fos = X[:, 3, :, :, :].rearrange("p h k n -> p (h k n)").rearrange("p (s h n) -> p s h n", s=KT // 2, h=2)
        rem_area = as_rows(3).rearrange("p (s n) -> p s n", n=H)
        rem_sum, rem_t = rem_area[:, 0, :], [rem_area[:, 1 + j, :] for j in range(NOTS)]
        rem_acc = Wt[:, :].bitcast(fp32).rearrange("p (s n) -> p s n", n=H)
        wt2s = rem_area[:, 3, :].rearrange("p (k n) -> p k n", k=MT1)
        t_out = acc[:, :, :].rearrange("p m n -> p (m n)").rearrange("p (s n) -> p s n", n=H)
        bnb = rows[:, 0, :]
        side_row = side[:, :, :].rearrange("p a n -> p (a n)")
        seen = [rows[:, 1, :], side_row]
        copied = [rows[:, 1, :], side_row]
        wt1ds, dens = side[0:D, 0, :], side[0:D, 1, :]

        mm = ctx.enter_context(nc.psum_tensor("mm", [P, RING, BLOCK], fp32))
        tp = ctx.enter_context(nc.psum_tensor("tp", [P, 2, BLOCK], fp32))
        tl = ctx.enter_context(nc.psum_tensor("tl", [P, 2, BLOCK], fp32))

        consts_in, smalls_in, ints_in = sem("consts_in"), sem("smalls_in"), sem("ints_in")
        bn2_in, wt_in = sem("bn2_in"), sem("wt_in")
        fold_in = [sem(f"fold_in{s}") for s in range(RING)]
        fo_out, fo_in = sem("fo_out"), sem("fo_in")
        wn1_in, wn2_in = sem("wn1_in"), sem("wn2_in")
        slice_in = [sem(f"slice_in{m}") for m in range(KT)]
        job_read, job_stored = sem("job_read"), sem("job_stored")
        top_in, dense_in, and_in, and_out = sem("top_in"), sem("dense_in"), sem("and_in"), sem("and_out")
        t_stored = [sem(f"t_stored{s}") for s in range(2)]
        y_out = sem("y_out")
        dve_step = sem("dve_step")
        idx_ready, bvec_ready = sem("idx_ready"), sem("bvec_ready")
        staged, pool_holds = sem("staged"), sem("pool_holds")
        sp_holds = sem("sp_holds")
        max_asked, max_known = sem("max_asked"), sem("max_known")
        scaled = sem("scaled")
        slot_scaled = sem("slot_scaled")
        job_scaled = sem("job_scaled")
        copy_done, hi_done, lo_done = sem("copy_done"), sem("hi_done"), sem("lo_done")
        job_hi, job_lo = sem("job_hi"), sem("job_lo")
        not_in = [sem(f"not_in{s}") for s in range(RT)]
        seen_in = [sem(f"seen_in{s}") for s in range(2)]
        seen_done = sem("seen_done")
        x_in = [sem(f"x_in{s}") for s in range(2)]
        row_in = [sem(f"row_in{s}") for s in range(2)]
        wt_out, wt_back = sem("wt_out"), sem("wt_back")
        rem_stored = [sem(f"rem_stored{s}") for s in range(2)]
        rem_in, rem_t_in = sem("rem_in"), [sem(f"rem_t_in{j}") for j in range(NOTS)]
        rem_step, rem_summed = sem("rem_step"), sem("rem_summed")
        mm_full = sem("mm_full")
        act_freed = sem("act_freed")
        dve_freed = sem("dve_freed")
        biased = sem("biased")
        h_split = sem("h_split")
        pair_step = sem("pair_step")
        turned = [sem("turned_a"), sem("turned_b")]
        high = [sem("high_a"), sem("high_b")]
        taken = [sem("taken_a"), sem("taken_b")]
        tl_full, tl_freed = sem("tl_full"), sem("tl_freed")
        h1_ready = sem("h1_ready")
        c1_ready, y_ready = sem("c1_ready"), sem("y_ready")
        acc_step = sem("acc_step")

        block = ctx.enter_context(nc.Block())

        @block.sync
        def _(sp):
            sp.dma_start(cst[:, :], consts).then_inc(consts_in, 16)
            sp.dma_start(scr[:, 0:TILES * F].bitcast(i32), ids).then_inc(ints_in, 16)
            sp.dma_start(scr[:, TILES * F:TILES * F + F].bitcast(i32),
                         fields.partition_broadcast(P)).then_inc(ints_in, 16)
            sp.dma_start(small[:, :], smalls).then_inc(smalls_in, 16)
            sp.dma_start(T32, wt1.rearrange("p (k n) -> p k n", k=KT)).then_inc(wt_in, 16)
            for n in range(G_FOLD):
                if n >= RING:
                    sp.wait_ge(mm_full, n - RING + 1)
                w = w2ta if n < KT else w2to
                sp.dma_start(fold_w[:, n % RING, :, :].rearrange("p k m -> p (k m)"), w[n % KT]).then_inc(fold_in[n % RING], 16)
                if n == 1:
                    sp.dma_start(W[:, 0:KT * 2 * H].bitcast(fp32), wn1).then_inc(wn1_in, 16)
                if n == RING:
                    sp.dma_start(W[:, KT * 2 * H:2 * KT * 2 * H].bitcast(fp32), wn2).then_inc(wn2_in, 16)
                    sp.dma_start(bnb, bn2.partition_broadcast(P)).then_inc(bn2_in, 16)
                    for q, s in enumerate(t_stored + [and_out, y_out, job_stored] + rem_stored):
                        sp.dma_start(token[q:q + 1, :], consts[0:1, 0:P]).then_inc(s, 16)
            sp.wait_ge(lo_done, IN_FO + KT // 2)
            sp.dma_start(fo_split, X[:, 3, :, :, :].rearrange("p h k n -> p (h k n)")).then_inc(fo_out, 16)
            sp.wait_ge(fo_out, 16)
            sp.wait_ge(lo_done, IN_WT + KT // 2)
            sp.dma_start(wt_split, Wt[:, :]).then_inc(wt_out, 16)
            def rem_store(i, t):
                sp.wait_ge(seen_done, i * SEEN + (1 + (t + 1) * F))
                sp.dma_start(rem_rows[bass.ds(i * BLOCK + t * P, P), :], rem_acc[:, t % 2, :]).then_inc(rem_stored[t % 2], 16)

            with sp.Fori(0, BLOCKS) as i:
                for j in range(NOTS):
                    for c in (2 * j, 2 * j + 1):
                        sp.wait_ge(job_lo, i * 4 + (c + 1))
                        sp.dma_start(job_in_f, pair_w[bass.ds(i * 4 + c, 1), :, :].rearrange("a p n -> (a p) n")).then_inc(job_read, 16)
                        sp.wait_ge(job_lo, i * 4 + (c + 2))
                        sp.dma_start(pair_split[bass.ds(i * 4 + c, 1), :, :].rearrange("a p n -> (a p) n"),
                                     job_out.rearrange("p h n -> p (h n)")).then_inc(job_stored, 16)
                    rem_store(i, 2 * j)
                    for bt in range(RT):
                        g = G0_NOT + j * 2 * KT + KT + 2 * bt + 1
                        sp.wait_ge(act_freed, i * G_NOT + (g + 1))
                        sp.dma_start(t_rows[bass.ds(i * BLOCK + (j * B + bt * P), P), :],
                                     t_out[:, bt % 2, :]).then_inc(t_stored[bt % 2], 16)
                    rem_store(i, 2 * j + 1)
            sp.wait_ge(job_stored, 16 * (1 + PAIR_SLICES))

            def pair_slice(m, q):
                sp.dma_start(W_pair[:, m, :, :].rearrange("p h n -> p (h n)"), pair_split[q]).then_inc(slice_in[m], 16)

            for m in range(KT):
                if m < KT // 2:
                    g = G0_NOT + (BLOCKS - 1) * G_NOT + 2 * KT + 2 * m + 1
                else:
                    g = G0_AND - 1
                sp.wait_ge(mm_full, g + 1)
                pair_slice(m, m)
            with sp.Fori(0, BLOCKS) as i:
                sp.wait_ge(act_freed, i * G_AND + (G0_AND + G_AND))
                sp.dma_start(and_dram[bass.ds(i * P, P), :],
                             acc[:, :, :].rearrange("p m n -> p (m n)")).then_inc(and_out, 16)
            for m in range(KT):
                sp.wait_ge(mm_full, G0_AND + (BLOCKS - 1) * G_AND + KT + m + 1)
                pair_slice(m, KT + m)
            sp.wait_ge(mm_full, G0_OR)
            sp.dma_start(Fw[:, :], fo_split).then_inc(fo_in, 16)
            sp.wait_ge(wt_out, 16)
            for s in range(2):
                sp.wait_ge(t_stored[s], T_STORES)
                sp.wait_ge(rem_stored[s], R_STORES)
            sp.dma_start(Wt[:, :], wt_split).then_inc(wt_back, 16)
            sp.dma_start(wt2s, wt2.rearrange("p (k n) -> p k n", k=MT1)).then_inc(top_in, 16)
            sp.dma_start(wt1ds, wt1d).then_inc(top_in, 16)
            sp.wait_ge(and_out, 16 * (1 + BLOCKS))

            def rem_load(i, t):
                sp.wait_ge(turned[1], i * R_OR + (R0_OR - 2 * RT if t == 0 else R0_OR + t))
                sp.dma_start(rem_sum, rem_rows[bass.ds(i * BLOCK + t * P, P), :]).then_inc(rem_in, 16)
                sp.wait_ge(rem_summed, i * RT + (t + 1))
                for j in range(NOTS):
                    sp.dma_start(rem_t[j], t_rows[bass.ds(i * BLOCK + (j * B + t * P), P), :]).then_inc(rem_t_in[j], 16)

            with sp.Fori(0, BLOCKS) as i:
                rem_load(i, 0)
                sp.wait_ge(tl_full, i * T_OR + 1)
                sp.wait_ge(y_out, i * 16 + 16)
                sp.sem_inc(sp_holds, 1)
                sp.dma_start(dens, dense_t[:, bass.ds(i * BLOCK, BLOCK)]).then_inc(dense_in, 16)
                sp.dma_start(acc[:, :, :].rearrange("p m n -> p (m n)"), and_dram[bass.ds(i * P, P), :]).then_inc(and_in, 16)
                for t in range(1, RT):
                    rem_load(i, t)
                sp.wait_ge(y_ready, i + 2)
                sp.dma_start(out.rearrange("b o -> o b")[:, bass.ds(i * BLOCK, BLOCK)], acc[0:1, 0, :]).then_inc(y_out, 16)
            sp.wait_ge(y_out, 16 * (1 + BLOCKS))

        @block.gpsimd
        def _(pool):
            def hold(what, value):
                pool.wait_ge(what, value)
                pool.sem_inc(pool_holds, 1)

            def gather(dst, source, bound, index):
                return pool.indirect_dma_start(dst, None, source, bass.IndirectOffsetOnAxis(ap=index, axis=0),
                                               bounds_check=bound, oob_is_err=False)

            def pair_row(tile, slot, buf, n, i=None, per=0):
                gather(rows[:, buf, :], table, ALL_ROWS - 1,
                       stage[:, tile // RT, tile % RT, C_PX + slot:C_PX + slot + 1]).then_inc(x_in[buf], 16)
                hold(x_in[buf], 16 * (n + 1) if i is None else i * per + 16 * (n + 1))
                gather(rows[:, buf, :], t_rows, NOTS * B - 1,
                       stage[:, tile // RT, tile % RT, C_PT + slot:C_PT + slot + 1]).then_inc(row_in[buf], 16)

            def over_partitions(c, n, asked, i=None, per=0):
                hold(max_asked, asked if i is None else i * per + asked)
                pool.partition_all_reduce(all_max[:, c:c + n], part_max[:, c:c + n], channels=P,
                                          reduce_op=MAX).then_inc(max_known, 1)

            hold(idx_ready, 1)
            for t in range(RT):
                gather(not_rows[:, t, :], table, ALL_ROWS - 1, idx[:, t, C_NOT:C_NOT + 1]).then_inc(not_in[t], 16)
            over_partitions(X_BN1, 4, 1)
            over_partitions(X_N2, 1, 2)
            over_partitions(X_FA, 1, 3)
            over_partitions(X_ROW, 1, 4)
            over_partitions(X_FO, 2, 5)
            with pool.Fori(0, BLOCKS) as i:
                for t in range(RT):
                    hold(not_in[t], i * (16 * NOTS) + 16)
                hold(seen_done, i * SEEN + 1)
                pool.tensor_copy(stage[:, 0, :, :], idx[:, bass.ds(i * RT, RT), :]).then_inc(staged, 1)
                pool.tensor_copy(stage[:, 1, :, :], idx[:, bass.ds(i * RT + RT, RT), :]).then_inc(staged, 1)
                hold(staged, i * 2 + 2)
                for j in range(NOTS):
                    asked = 5 + 3 * j
                    for t in range(RT):
                        hold(turned[1], i * R_NOT + (j * RT + t + 1))
                        gather(not_rows[:, t, :], table, ALL_ROWS - 1,
                               stage[:, j, t, C_NOT + 1 - j:C_NOT + 2 - j]).then_inc(not_in[t], 16)
                    for k in range(SEEN // NOTS):
                        if k in (0, 3, 6):
                            col = (X_JOB, X_JOB + 1, X_ROW + 1 - j)[k // 3]
                            over_partitions(col, 1, asked + k // 3 + 1, i, 3 * NOTS)
                        n = j * (SEEN // NOTS) + k
                        t, f = n // F, n % F
                        if n < 2:
                            hold(seen_done, i * SEEN + 1)
                        else:
                            hold(seen_done, i * SEEN + n)
                        gather(seen[n % 2], table, ALL_ROWS - 1,
                               stage[:, 0, t, C_ALL + f:C_ALL + f + 1]).then_inc(seen_in[n % 2], 16)
            over_partitions(X_ALL, 1, 5 + 3 * NOTS * BLOCKS + 1)

            for s in range(2):
                hold(t_stored[s], T_STORES)
            for t in range(RT):
                hold(not_in[t], 16 * (1 + NOTS * BLOCKS))
            pool.tensor_copy(stage[:, 0, :, :], idx[:, 0:RT, :]).then_inc(staged, 1)
            hold(staged, 2 * BLOCKS + 1)
            for n in range(2 * RT):
                if n >= 2:
                    hold(turned[1], R0_AND - 2 * RT + n - 1)
                pair_row(n % RT, n // RT, n % 2, n // 2)
            with pool.Fori(0, BLOCKS) as i:
                for s in range(2):
                    hold(row_in[s], i * (16 * R_AND // 2) + 16 * RT)
                pool.tensor_copy(stage[:, 0, :, :], idx[:, bass.ds(i * RT, RT), :]).then_inc(staged, 1)
                pool.tensor_copy(stage[:, 1, :, :], idx[:, bass.ds(i * RT + RT, RT), :]).then_inc(staged, 1)
                hold(staged, i * 2 + (2 * BLOCKS + 3))
                for n in range(R_AND):
                    hold(turned[1], i * R_AND + (R0_AND + n - 1))
                    pair = 1 - n // (2 * RT)
                    pair_row((1 - pair) * RT + n % RT, 2 * pair + n // RT % 2, n % 2,
                             RT + n // 2, i, 16 * R_AND // 2)
            used = RT + BLOCKS * R_AND // 2
            for s in range(2):
                hold(row_in[s], 16 * used)
            pool.tensor_copy(stage[:, 0, :, :], idx[:, 0:RT, :]).then_inc(staged, 1)
            hold(staged, 4 * BLOCKS + 2)
            for n in range(2 * RT):
                hold(turned[1], R0_OR - 2 * RT + n - 1)
                pair_row(n % RT, 2 * AND_PAIRS + n // RT, n % 2, used + n // 2)
            with pool.Fori(0, BLOCKS) as i:
                for s in range(2):
                    hold(row_in[s], i * (16 * RT) + 16 * (used + RT))
                pool.tensor_copy(stage[:, 0, :, :], idx[:, bass.ds(i * RT, RT), :]).then_inc(staged, 1)
                pool.tensor_copy(stage[:, 1, :, :], idx[:, bass.ds(i * RT + RT, RT), :]).then_inc(staged, 1)
                hold(staged, i * 2 + (4 * BLOCKS + 4))
                for n in range(2 * RT):
                    hold(turned[1], i * R_OR + (R0_OR + (RT if n > 1 else 0) + n - 1))
                    pair_row(RT + n % RT, 2 * AND_PAIRS + n // RT, n % 2, used + RT + n // 2, i, 16 * RT)

        @block.tensor
        def _(pe):
            pe.wait_ge(consts_in, 16)
            pe.wait_ge(wt_in, 16)

            def turn(src, r, i=None, per=0):
                for h in range(2):
                    if i is not None or r:
                        pe.wait_ge(taken[h], r if i is None else i * per + r)
                    for k in range(KT // 2):
                        kk = h * (KT // 2) + k
                        last = pe.transpose(tp[:, h, k * P:(k + 1) * P], src[:, kk * P:(kk + 1) * P], ident)
                    last.then_inc(turned[h], 1)

            def products(bank, pairs):
                n = 0
                for a, b in pairs:
                    for pa, pb in ((0, 0), (0, 1), (1, 0)):
                        last = pe.matmul(bank, a(pa), b(pb), start=(n == 0), stop=(n == 3 * len(pairs) - 1))
                        n += 1
                return last

            for n in range(G_FOLD):
                pe.wait_ge(fold_in[n % RING], 16 * (n // RING + 1))
                if n >= RING:
                    pe.wait_ge(act_freed, n - RING + 1)
                for k in range(KT):
                    last = pe.matmul(mm[:, n % RING, :], fold_w[:, n % RING, k, :], T32[:, k, :],
                                     start=(k == 0), stop=(k == KT - 1))
                last.then_inc(mm_full, 1)
            pe.wait_ge(bvec_ready, 1)
            for m in range(MT1):
                for k in range(KT):
                    last = pe.matmul(tl[:, 0, m:m + 1], T32[:, k, m * P:(m + 1) * P], bvec[:, k:k + 1],
                                     start=(k == 0), stop=(k == KT - 1))
            last.then_inc(tl_full, 1)

            for t in range(RT):
                pe.wait_ge(not_in[t], 16)
                turn(not_rows[:, t, :], t)
            with pe.Fori(0, BLOCKS) as i:
                for j in range(NOTS):
                    for h in range(2):
                        pe.wait_ge(taken[h], i * R_NOT + (R0_NOT + j * RT))
                    if j == 0:
                        pe.wait_ge(lo_done, IN_N2)
                    for m in range(KT):
                        g = G0_NOT + j * 2 * KT + m
                        pe.wait_ge(act_freed, i * G_NOT + (g - RING + 1))
                        products(mm[:, g % RING, :],
                                 [(lambda h, k=k: W_not[:, m, h, k * P:(k + 1) * P],
                                   lambda h, k=k: X[:, j, h, k, :]) for k in range(KT)]).then_inc(mm_full, 1)
                    if j == 0:
                        pe.wait_ge(lo_done, IN_N2 + KT)
                    for bt in range(RT):
                        pe.wait_ge(not_in[bt], i * (16 * NOTS) + 16 * (j + 2))
                        turn(not_rows[:, bt, :], R0_NOT + j * RT + bt, i, R_NOT)
                        if bt == 0:
                            pe.wait_ge(h_split, i * (NOTS * KT) + (j * KT + KT + 1))
                        for nh in range(2):
                            g = G0_NOT + j * 2 * KT + KT + 2 * bt + nh
                            pe.wait_ge(act_freed, i * G_NOT + (g - RING + 1))
                            products(mm[:, g % RING, :],
                                     [(lambda h, k=k: Hb[:, h, k, bt * P:(bt + 1) * P],
                                       lambda h, k=k: W_not[:, KT + k, h, nh * HALF:(nh + 1) * HALF])
                                      for k in range(KT)]).then_inc(mm_full, 1)

            def pair_group(bank, m, s0):
                return products(mm[:, bank, :],
                                [(lambda h, k=k: W_pair[:, m, h, k * P:(k + 1) * P],
                                  lambda h, k=k: X[:, s0 + k // KT, h, k % KT, :]) for k in range(2 * KT)])

            def top_group(bank, m, weights, x):
                return products(mm[:, bank, :],
                                [(lambda h, k=k: weights[:, k // 2, h, (k % 2) * M1 + m * P:(k % 2) * M1 + (m + 1) * P],
                                  lambda h, k=k: x[:, h, k, :]) for k in range(KT)])

            for n in range(2 * RT):
                pe.wait_ge(row_in[n % 2], 16 * (n // 2 + 1))
                turn(rows[:, n % 2, :], R0_AND - 2 * RT + n)
            with pe.Fori(0, BLOCKS) as i:
                for pair in range(AND_PAIRS):
                    for h in range(2):
                        pe.wait_ge(taken[h], i * R_AND + (R0_AND + pair * 2 * RT))
                    for m in range(KT):
                        g = G0_AND + pair * KT + m
                        pe.wait_ge(slice_in[m], 16)
                        pe.wait_ge(act_freed, i * G_AND + (g - RING + 1))
                        pair_group(g % RING, m, 2 * pair).then_inc(mm_full, 1)
                        n = pair * 2 * RT + m
                        pe.wait_ge(row_in[n % 2], i * (16 * R_AND // 2) + 16 * (RT + n // 2 + 1))
                        turn(rows[:, n % 2, :], R0_AND + n, i, R_AND)
                pe.wait_ge(h_split, i * (2 * KT) + (SPLIT_NOT + 2 * KT))
                for m in range(MT1):
                    g = G0_AND + AND_PAIRS * KT + m
                    pe.wait_ge(act_freed, i * G_AND + (g - RING + 1))
                    top_group(g % RING, m, Fs, Hb).then_inc(mm_full, 1)

            used = RT + BLOCKS * R_AND // 2
            for n in range(2 * RT):
                pe.wait_ge(row_in[n % 2], 16 * (used + n // 2 + 1))
                turn(rows[:, n % 2, :], R0_OR - 2 * RT + n)
            pe.wait_ge(act_freed, G0_OR)
            pe.wait_ge(fo_in, 16)
            pe.wait_ge(top_in, 32)
            pe.wait_ge(wt_back, 16)
            with pe.Fori(0, BLOCKS) as i:
                for h in range(2):
                    pe.wait_ge(taken[h], i * R_OR + R0_OR)
                for m in range(KT):
                    pe.wait_ge(slice_in[m], 32)
                    if m < RING:
                        pe.wait_ge(dve_freed, i * (2 * MT1) + (MT1 + m + 1))
                    else:
                        pe.wait_ge(act_freed, i * KT + (G0_OR + m - RING + 1))
                    pair_group(m % RING, m, 0).then_inc(mm_full, 1)
                    if m % 2:
                        pe.wait_ge(rem_summed, i * RT + (m // 2 + 2))
                        turn(rem_sum, R0_OR + m // 2, i, R_OR)
                pe.wait_ge(h_split, i * KT + (SPLIT_AND + KT))
                for h in range(2):
                    pe.wait_ge(taken[h], i * R_OR + (R0_OR + RT))
                pe.wait_ge(dense_in, i * 16 + 16)
                for m in range(MT1):
                    for q, (weights, x) in enumerate(((Fs, Hb), (Ts, X[:, 2, :, :, :]))):
                        n = 2 * m + q
                        if n < RING:
                            pe.wait_ge(act_freed, i * KT + (G0_OR + KT - RING + n + 1))
                        else:
                            pe.wait_ge(dve_freed, i * (2 * MT1) + (2 * MT1 + n - RING + 1))
                        top_group(n % RING, m, weights, x).then_inc(mm_full, 1)
                    pe.wait_ge(tl_freed, i * T_OR + max(m, 1))
                    pe.matmul(tl[:, m % 2, :], wt1ds[:, m * P:(m + 1) * P], dens,
                              start=True, stop=True).then_inc(tl_full, 1)
                    for n in (2 * m, 2 * m + 1):
                        pe.wait_ge(row_in[n % 2], i * (16 * RT) + 16 * (used + RT + n // 2 + 1))
                        turn(rows[:, n % 2, :], R0_OR + RT + n, i, R_OR)
                pe.wait_ge(h1_ready, i * MT1 + MT1)
                for m in range(MT2):
                    pe.wait_ge(tl_freed, i * T_OR + (MT1 + m))
                    for k in range(MT1):
                        last = pe.matmul(tl[:, m % 2, :], wt2s[:, k, m * P:(m + 1) * P], acc[:, k, :],
                                         start=(k == 0), stop=(k == MT1 - 1))
                    last.then_inc(tl_full, 1)
                pe.wait_ge(tl_freed, i * T_OR + (MT1 + MT2 + 1))
                for k in range(MT2):
                    last = pe.matmul(tl[0:1, 0, :], small[:, S_W3 + k:S_W3 + k + 1], tmp[:, k, :],
                                     start=(k == 0), stop=(k == MT2 - 1))
                last.then_inc(tl_full, 1)

        @block.scalar
        def _(act):
            A = nc.scalar.activation

            def take(r, slot, t, scale, i=None, per=0):
                for h in range(2):
                    act.wait_ge(turned[h], (r if i is None else i * per + r) + 1)
                    A(X[:, slot, 0, h * KT // 2:(h + 1) * KT // 2, t * P:(t + 1) * P],
                      tp[:, h, :].rearrange("p (k b) -> p k b", k=KT // 2),
                      ACT.Copy, scale=up[:, scale:scale + 1]).then_inc(high[h], 1)

            def fold_out(n):
                act.wait_ge(mm_full, n + 1)
                dst = F32[:, n, :] if n < KT else Fo32[:, n - KT, :]
                A(dst, mm[:, n % RING, :], ACT.Copy).then_inc(act_freed, 1)

            def split_in_place(n, hi, whole, scale, ready):
                act.wait_ge(scaled, ready)
                if n >= 2:
                    act.wait_ge(lo_done, n - 1)
                A(copied[n % 2], whole, ACT.Copy).then_inc(copy_done, 1)
                act.wait_ge(copy_done, n + 1)
                A(hi, copied[n % 2], ACT.Copy, scale=up[:, scale:scale + 1]).then_inc(hi_done, 1)

            def slice_of(n):
                if n < IN_FA:
                    return W_not[:, n, 0, :], W_not[:, n, :, :].rearrange("p h n -> p (h n)").bitcast(fp32), \
                        (U_N1 if n < KT else U_N2), (1 if n < KT else 2)
                src, c, base, ready = ((Fs, U_FA, IN_FA, 3) if n < IN_FO else
                                       (Fos, U_FO, IN_FO, 5) if n < IN_WT else (Ts, U_WT, IN_WT, 5))
                v = src[:, n - base, :, :]
                return v[:, 0, :], v.rearrange("p h n -> p (h n)").bitcast(fp32), c, ready

            def split(n):
                hi, whole, scale, ready = slice_of(n)
                split_in_place(n, hi, whole, scale, ready)

            for n in range(RING):
                fold_out(n)
            for n in range(KT):
                split(n)
                fold_out(RING + n)
            for n in range(KT):
                split(KT + n)
                if n < RING:
                    fold_out(RING + KT + n)
            for n in range(IN_FA, IN_FO):
                split(n)
            act.wait_ge(slot_scaled, 1)
            for t in range(RT):
                take(t, 0, t, U_X)
            act.wait_ge(tl_full, 1)
            for n in range(IN_FO, IN_WT + KT // 2):
                split(n)
            act.wait_ge(fo_out, 16)

            def job(i, c):
                act.wait_ge(job_scaled, i * 4 + (c + 1))
                act.wait_ge(job_stored, i * 64 + 16 * (c + 1))
                A(job_out[:, 0, :], job_in_f, ACT.Copy,
                  scale=up[:, U_JOB + c % 2:U_JOB + c % 2 + 1]).then_inc(job_hi, 1)

            with act.Fori(0, BLOCKS) as i:
                for j in range(NOTS):
                    for m in range(KT):
                        g = G0_NOT + j * 2 * KT + m
                        act.wait_ge(mm_full, i * G_NOT + (g + 1))
                        act.wait_ge(h_split, i * (NOTS * KT) + max(j * KT + m, 1))
                        for dst in (Hb[:, 0, m, :], tmp[:, m % 2, :]):
                            last = A(dst, mm[:, g % RING, :], ACT.Relu, bias=b_not[:, j, m:m + 1],
                                     scale=u[:, V_NOT1 + j:V_NOT1 + j + 1])
                        last.then_inc(act_freed, 1)
                        if m in (2, 5):
                            job(i, 2 * j + m // 3)
                    act.wait_ge(slot_scaled, i * NOTS + (j + 2))
                    for bt in range(RT):
                        take(R0_NOT + j * RT + bt, 1 - j, bt, U_X + 1 - j, i, R_NOT)
                        act.wait_ge(t_stored[bt % 2], i * (16 * NOTS * RT // 2) + 16 * (1 + j * RT // 2 + bt // 2))
                        for nh in range(2):
                            g = G0_NOT + j * 2 * KT + KT + 2 * bt + nh
                            act.wait_ge(biased, i * (NOTS * KT) + (j * KT + 2 * bt + nh + 1))
                            A(t_out[:, bt % 2, nh * HALF:(nh + 1) * HALF], mm[:, g % RING, :],
                              ACT.Tanh).then_inc(act_freed, 1)
            for s in range(2):
                act.wait_ge(t_stored[s], T_STORES)
            act.wait_ge(scaled, 6)
            for n in range(2 * RT):
                take(R0_AND - 2 * RT + n, n // RT, n % RT, U_ALL)
            with act.Fori(0, BLOCKS) as i:
                for pair in range(AND_PAIRS):
                    for m in range(KT):
                        g = G0_AND + pair * KT + m
                        act.wait_ge(mm_full, i * G_AND + (g + 1))
                        act.wait_ge(h_split, i * (2 * KT) + (SPLIT_NOT + pair * KT + m - 1))
                        dsts = ((Hb[:, 0, m, :],) if pair == 0 else ()) + (tmp[:, m % 2, :],)
                        for dst in dsts:
                            last = A(dst, mm[:, g % RING, :], ACT.Relu, bias=b_pair[:, 0, m:m + 1],
                                     scale=u_pair[:, m:m + 1])
                        last.then_inc(act_freed, 1)
                        n = pair * 2 * RT + m
                        take(R0_AND + n, 2 * (1 - pair) + m // RT, m % RT, U_ALL, i, R_AND)
                act.wait_ge(and_out, i * 16 + 16)
                for m in range(MT1):
                    g = G0_AND + AND_PAIRS * KT + m
                    act.wait_ge(mm_full, i * G_AND + (g + 1))
                    A(acc[:, m, :], mm[:, g % RING, :], ACT.Copy,
                      scale=u[:, V_TOPA:V_TOPA + 1]).then_inc(act_freed, 1)
            for n in range(2 * RT):
                take(R0_OR - 2 * RT + n, n // RT, n % RT, U_ALL)
            with act.Fori(0, BLOCKS) as i:
                for m in range(KT):
                    act.wait_ge(mm_full, i * G_OR + (G0_OR + m + 1))
                    if m == 0:
                        act.wait_ge(y_ready, i + 1)
                    act.wait_ge(h_split, i * KT + (SPLIT_AND + m - 1))
                    for dst in (Hb[:, 0, m, :], tmp[:, m % 2, :]):
                        last = A(dst, mm[:, m % RING, :], ACT.Relu, bias=b_pair[:, 1, m:m + 1],
                                 scale=u_pair[:, KT + m:KT + m + 1])
                    last.then_inc(act_freed, 1)
                    if m % 2:
                        take(R0_OR + m // 2, 2, m // 2, U_REM, i, R_OR)
                for m in range(MT1):
                    for n in (2 * m, 2 * m + 1):
                        take(R0_OR + RT + n, n // RT, n % RT, U_ALL, i, R_OR)
                    act.wait_ge(acc_step, i * (3 * MT1) + (3 * m + 3))
                    A(acc[:, m, :], acc[:, m, :], ACT.Relu, bias=c1[:, m:m + 1]).then_inc(h1_ready, 1)
                for m in range(MT2):
                    act.wait_ge(tl_full, i * T_OR + (1 + MT1 + m + 1))
                    A(tmp[:, m, :], tl[:, m % 2, :], ACT.Relu,
                      bias=small[:, S_T2 + m:S_T2 + m + 1]).then_inc(tl_freed, 1)
                act.wait_ge(tl_full, i * T_OR + (1 + T_OR))
                A(acc[0:1, 0, :], tl[0:1, 0, :], ACT.Copy).then_inc(y_ready, 1)
                act.wait_ge(y_ready, i + 2)
                act.sem_inc(tl_freed, 1)

        @block.vector
        def _(dve):
            V = nc.vector
            steps = [0]

            def step(ins, i=None, per=0):
                steps[0] += 1
                ins.then_inc(dve_step, 1)
                dve.wait_ge(dve_step, steps[0] if i is None else i * per + steps[0])

            dve.sem_inc(dve_freed, 2 * MT1)
            dve.sem_inc(tl_freed, 1)
            dve.sem_inc(rem_summed, 1)
            dve.sem_inc(seen_done, 1)
            dve.sem_inc(h_split, 1)
            dve.sem_inc(job_lo, 1)
            dve.sem_inc(y_ready, 1)
            dve.wait_ge(consts_in, 16)
            dve.wait_ge(ints_in, 32)
            at = [TILES * F + F]

            def scratch(*shape):
                n = int(np.prod(shape))
                v = scr[:, at[0]:at[0] + n]
                at[0] += n
                if len(shape) == 2:
                    v = v.rearrange("p (a b) -> p a b", a=shape[0])
                return v

            ids_i = scr[:, 0:TILES * F].bitcast(i32).rearrange("p (t f) -> p t f", f=F)
            fields_i = scr[:, TILES * F:TILES * F + F].bitcast(i32)
            Q = NOTS + SLOTS
            which, neg = scratch(Q), scratch(Q)
            loc, wrap, prod = scratch(TILES, F), scratch(TILES, F), scratch(TILES, F)
            eq, row = scratch(Q, F), scratch(TILES, Q)
            notf, used, rest, valid = scratch(F), scratch(F), scratch(F), scratch(F)
            e6 = scratch(SLOTS, F)
            isn, in0, keep, trow = scratch(SLOTS), scratch(SLOTS), scratch(SLOTS), scratch(SLOTS)
            cnt, e2 = scratch(1), scratch(NOTS, F)
            idxf = scratch(TILES, COLS)
            field_no, start, last_id = (cst[:, k:k + F] for k in (K_FIELD, K_START, K_LAST))
            batch_no = cst[:, K_ROW:K_ROW + TILES]

            def over_tiles(v, n):
                return v.unsqueeze(1).to_broadcast([P, TILES, n])

            step(V.tensor_copy(which, fields_i))
            step(V.tensor_scalar(neg, which, 0.0, float(F), ALU.is_lt, ALU.mult))
            step(V.tensor_tensor(which, which, neg, ALU.add))
            step(V.tensor_copy(loc, ids_i))
            step(V.tensor_scalar(wrap, loc, 0.0, None, ALU.is_lt))
            step(V.tensor_tensor(prod, wrap, over_tiles(last_id, F), ALU.mult))
            step(V.tensor_tensor(loc, loc, prod, ALU.add))
            step(V.tensor_tensor(loc, loc, wrap, ALU.add))
            step(V.tensor_scalar(loc, loc, 0.0, None, ALU.max))
            step(V.tensor_tensor(loc, loc, over_tiles(last_id, F), ALU.min))
            step(V.tensor_tensor(loc, loc, over_tiles(start, F), ALU.add))
            step(V.tensor_tensor(eq, field_no.unsqueeze(1).to_broadcast([P, Q, F]),
                                 which.unsqueeze(2).to_broadcast([P, Q, F]), ALU.is_equal))
            for q in range(Q):
                step(V.tensor_tensor(prod, loc, over_tiles(eq[:, q, :], F), ALU.mult))
                step(V.tensor_reduce(row[:, :, q:q + 1], prod, AX.X, ALU.add))
            step(V.tensor_tensor(notf, eq[:, 0, :], eq[:, 1, :], ALU.max))
            pairs = eq[:, NOTS:Q, :]
            step(V.tensor_tensor(e6, pairs, notf.unsqueeze(1).to_broadcast([P, SLOTS, F]), ALU.mult))
            step(V.tensor_reduce(isn, e6, AX.X, ALU.add))
            step(V.tensor_tensor(e6, pairs, eq[:, 0, :].unsqueeze(1).to_broadcast([P, SLOTS, F]), ALU.mult))
            step(V.tensor_reduce(in0, e6, AX.X, ALU.add))
            step(V.tensor_reduce(used, pairs.rearrange("p q f -> p f q"), AX.X, ALU.max))
            step(V.tensor_scalar(rest, used, -1.0, 1.0, ALU.mult, ALU.add))
            step(V.tensor_reduce(cnt, rest, AX.X, ALU.add))
            step(V.tensor_scalar(cnt, cnt, float(AND_PAIRS + OR_PAIRS), None, ALU.add))
            step(V.reciprocal(invc[:, :], cnt))
            step(V.tensor_copy(idxf[:, :, C_NOT:C_NOT + NOTS], row[:, :, 0:NOTS]))
            step(V.tensor_copy(idxf[:, :, C_ALL:C_ALL + F], loc))

            def masked(cols, n, rows_ap, mask):
                dst = idxf[:, :, cols:cols + n]
                step(V.tensor_scalar(dst, rows_ap, -float(SKIP), None, ALU.add))
                step(V.tensor_tensor(dst, dst, over_tiles(mask, n), ALU.mult))
                step(V.tensor_scalar(dst, dst, float(SKIP), None, ALU.add))

            step(V.tensor_scalar(keep, isn, -1.0, 1.0, ALU.mult, ALU.add))
            masked(C_PX, SLOTS, row[:, :, NOTS:Q], keep)
            step(V.tensor_scalar(trow, in0, -float(B), float(B), ALU.mult, ALU.add))
            tr = idxf[:, :, C_PT:C_PT + SLOTS]
            step(V.tensor_tensor(tr, batch_no.unsqueeze(2).to_broadcast([P, TILES, SLOTS]),
                                 over_tiles(trow, SLOTS), ALU.add))
            masked(C_PT, SLOTS, tr, isn)
            step(V.tensor_scalar(valid, notf, -1.0, 1.0, ALU.mult, ALU.add))
            step(V.tensor_tensor(valid, valid, rest, ALU.mult))
            step(V.tensor_copy(rem_w[:, 0:F], valid))
            step(V.tensor_tensor(e2[:, 0, :], rest, eq[:, 0, :], ALU.mult))
            step(V.tensor_tensor(e2[:, 1, :], rest, eq[:, 1, :], ALU.mult))
            step(V.tensor_scalar(valid, eq[:, 0, :], -1.0, 1.0, ALU.mult, ALU.add))
            step(V.tensor_tensor(e2[:, 1, :], e2[:, 1, :], valid, ALU.mult))
            step(V.tensor_reduce(rem_w[:, F:F + NOTS], e2, AX.X, ALU.add))
            step(V.tensor_copy(idx[:, 0:TILES, :], idxf))
            V.tensor_copy(idx[:, TILES:TILES + RT, :], idxf[:, 0:RT, :]).then_inc(idx_ready, 1)

            dve.wait_ge(smalls_in, 16)
            step(V.tensor_scalar(bvec[:, :], small[:, S_A2:S_A2 + KT], float(AND_PAIRS), None, ALU.mult))
            V.scalar_tensor_tensor(out=bvec[:, :], in0=small[:, S_O2:S_O2 + KT], scalar=float(OR_PAIRS),
                                   in1=bvec[:, :], op0=ALU.mult, op1=ALU.add).then_inc(bvec_ready, 1)

            asked = [0]

            def largest(dst, src):
                return V.tensor_reduce(dst, src, AX.X, ALU.max, apply_absolute_value=True)

            def col(t, c):
                return t[:, c:c + 1]

            def scale_from(c, value, i=None, per=0):
                step(V.tensor_scalar(col(down, c), value, LEAST, None, ALU.max), i, per)
                step(V.tensor_scalar(col(down, c).bitcast(i32), col(down, c).bitcast(i32), EXPONENT, None,
                                     ALU.bitwise_and), i, per)
                step(V.tensor_scalar(col(down, c), col(down, c), 2.0 ** -14, None, ALU.mult), i, per)
                step(V.reciprocal(col(up, c), col(down, c)), i, per)

            def sized(c, slices):
                for n, v in enumerate(slices):
                    largest(col(piece, n), v).then_inc(dve_step, 1)
                    steps[0] += 1
                dve.wait_ge(dve_step, steps[0])
                step(V.tensor_reduce(col(part_max, c), piece[:, 0:len(slices)], AX.X, ALU.max))

            def ask():
                asked[0] += 1
                dve.sem_inc(max_asked, 1)

            def f32_slices(v, n):
                return [v[:, s, :, :].rearrange("p h n -> p (h n)").bitcast(fp32) for s in n]

            def split_scale(n):
                return U_N1 if n < IN_N2 else U_N2 if n < IN_FA else U_FA if n < IN_FO else U_FO if n < IN_WT else U_WT

            def lo_in_place(n, v):
                dve.wait_ge(hi_done, n + 1)
                V.scalar_tensor_tensor(out=v[:, 1, :], in0=copied[n % 2], scalar=col(up, split_scale(n)), in1=v[:, 0, :],
                                       op0=ALU.mult, op1=ALU.subtract).then_inc(lo_done, 1)

            for c, k in ((X_BN1, S_N1), (X_BA1, S_A1), (X_BO1, S_O1)):
                step(largest(col(part_max, c), small[:, k:k + KT]))
            dve.wait_ge(wn1_in, 16)
            sized(X_N1, f32_slices(W_not, range(KT)))
            ask()
            dve.wait_ge(max_known, 1)
            scale_from(U_N1, col(all_max, X_N1))
            dve.sem_inc(scaled, 1)
            step(V.tensor_scalar(col(u, V_BOUND), col(all_max, X_N1), float(H), None, ALU.mult))
            for n in range(KT):
                lo_in_place(n, W_not[:, n, :, :])
            dve.wait_ge(wn2_in, 16)
            sized(X_N2, f32_slices(W_not, range(KT, 2 * KT)))
            ask()
            dve.wait_ge(max_known, 2)
            scale_from(U_N2, col(all_max, X_N2))
            dve.sem_inc(scaled, 1)
            for n in range(KT, 2 * KT):
                lo_in_place(n, W_not[:, n, :, :])
            dve.wait_ge(act_freed, KT)
            sized(X_FA, f32_slices(Fs, range(KT // 2)))
            ask()
            dve.wait_ge(max_known, 3)
            scale_from(U_FA, col(all_max, X_FA))
            dve.sem_inc(scaled, 1)
            for n in range(KT // 2):
                lo_in_place(IN_FA + n, Fs[:, n, :, :])

            def slot_scales(j, i=None, per=0):
                scale_from(U_X + j, col(all_max, X_ROW + j), i, per)
                bound = col(piece, 15)
                step(V.scalar_tensor_tensor(out=bound, in0=col(all_max, X_ROW + j), scalar=col(u, V_BOUND),
                                            in1=col(all_max, X_BN1), op0=ALU.mult, op1=ALU.add), i, per)
                scale_from(U_H + j, bound, i, per)
                step(V.tensor_scalar(b_not[:, j, :], small[:, S_N1:S_N1 + KT], col(up, U_H + j), None, ALU.mult), i, per)
                step(V.scalar_tensor_tensor(out=col(u, V_NOT1 + j), in0=col(up, U_H + j), scalar=col(down, U_X + j),
                                            in1=col(down, U_N1), op0=ALU.mult, op1=ALU.mult), i, per)
                step(V.tensor_tensor(col(u, V_NOT2 + j), col(down, U_H + j), col(down, U_N2), ALU.mult), i, per)
                dve.sem_inc(slot_scaled, 1)

            for t in range(RT):
                dve.wait_ge(not_in[t], 16)
            sized(X_ROW, [not_rows[:, t, :] for t in range(RT)])
            ask()
            dve.wait_ge(max_known, 4)
            slot_scales(0)

            def take(r, slot, t, scale, i=None, per=0):
                for h in range(2):
                    half = slice(h * KT // 2, (h + 1) * KT // 2)
                    dve.wait_ge(high[h], (r if i is None else i * per + r) + 1)
                    V.scalar_tensor_tensor(out=X[:, slot, 1, half, t * P:(t + 1) * P],
                                           in0=tp[:, h, :].rearrange("p (k b) -> p k b", k=KT // 2),
                                           scalar=col(up, scale),
                                           in1=X[:, slot, 0, half, t * P:(t + 1) * P],
                                           op0=ALU.mult, op1=ALU.subtract).then_inc(taken[h], 1)

            for t in range(RT):
                take(t, 0, t, U_X)
            dve.wait_ge(tl_full, 1)
            V.scalar_tensor_tensor(out=c1[:, :], in0=tl[:, 0, 0:MT1], scalar=invc[:, 0:1],
                                   in1=small[:, S_T1:S_T1 + MT1], op0=ALU.mult, op1=ALU.add).then_inc(c1_ready, 1)
            dve.wait_ge(act_freed, G_FOLD)
            sized(X_FO, f32_slices(Fos, range(KT // 2)))
            sized(X_WT, f32_slices(Ts, range(KT // 2)))
            ask()
            dve.wait_ge(max_known, 5)
            scale_from(U_FO, col(all_max, X_FO))
            scale_from(U_WT, col(all_max, X_WT))
            dve.sem_inc(scaled, 2)
            for n in range(KT // 2):
                lo_in_place(IN_FO + n, Fos[:, n, :, :])
            for n in range(KT // 2):
                lo_in_place(IN_WT + n, Ts[:, n, :, :])
            step(V.memset(field_run[:, :], 1.0))
            dve.wait_ge(bn2_in, 16)
            dve.wait_ge(wt_out, 16)

            def hidden_lo(m, count, i, per):
                dve.wait_ge(act_freed, i * per + count)
                V.tensor_tensor(Hb[:, 1, m, :], tmp[:, m % 2, :], Hb[:, 0, m, :], ALU.subtract).then_inc(h_split, 1)

            def see(i, n):
                dve.wait_ge(seen_in[n % 2], i * (16 * SEEN // 2) + 16 * (n // 2 + 1))
                largest(col(piece, n % (SEEN // NOTS)) if n % (SEEN // NOTS) < 15 else col(field_run, 1),
                        seen[n % 2])
                t, f = n // F, n % F
                total = rem_acc[:, t % 2, :]
                if f == 0:
                    dve.wait_ge(rem_stored[t % 2], i * (16 * RT // 2) + 16 * (1 + t // 2))
                    V.tensor_scalar(total, seen[n % 2], col(rem_w, f), None, ALU.mult).then_inc(seen_done, 1)
                else:
                    dve.wait_ge(seen_done, i * SEEN + (n + 1))
                    V.scalar_tensor_tensor(out=total, in0=seen[n % 2], scalar=col(rem_w, f), in1=total,
                                           op0=ALU.mult, op1=ALU.add).then_inc(seen_done, 1)

            base = steps[0]
            PER = NOT_STEPS
            with dve.Fori(0, BLOCKS) as i:
                for j in range(NOTS):
                    def ask_for(k):
                        dve.sem_inc(max_asked, 1)

                    def known(k):
                        dve.wait_ge(max_known, i * (3 * NOTS) + (5 + 3 * j + k + 1))

                    def job_max(c):
                        dve.wait_ge(job_read, i * 64 + 16 * (c + 1))
                        step(largest(col(part_max, X_JOB + c % 2), job_in_f), i, PER)
                        ask_for(c % 2)

                    def job_scale(c):
                        known(c % 2)
                        scale_from(U_JOB + c % 2, col(all_max, X_JOB + c % 2), i, PER)
                        step(V.tensor_copy(slice_max[:, bass.ds(i * 4 + c, 1)], col(all_max, X_JOB + c % 2)), i, PER)
                        step(V.tensor_copy(slice_down[:, bass.ds(i * 4 + c, 1)], col(down, U_JOB + c % 2)), i, PER)
                        dve.sem_inc(job_scaled, 1)

                    def job_rest(c):
                        dve.wait_ge(job_hi, i * 4 + (c + 1))
                        V.scalar_tensor_tensor(out=job_out[:, 1, :], in0=job_in_f, scalar=col(up, U_JOB + c % 2),
                                               in1=job_out[:, 0, :], op0=ALU.mult, op1=ALU.subtract).then_inc(job_lo, 1)

                    for m in range(KT):
                        hidden_lo(m, G0_NOT + j * 2 * KT + m + 1, i, G_NOT)
                        if m in (0, 3):
                            job_max(2 * j + m // 3)
                        if m in (1, 4):
                            job_scale(2 * j + m // 3)
                        if m in (2, 5):
                            job_rest(2 * j + m // 3)
                        if m == 5:
                            for t in range(RT):
                                dve.wait_ge(not_in[t], i * (16 * NOTS) + 16 * (j + 2))
                                step(largest(col(rowmax, t), not_rows[:, t, :]), i, PER)
                            step(V.tensor_reduce(col(part_max, X_ROW + 1 - j), rowmax[:, 0:RT], AX.X, ALU.max), i, PER)
                            ask_for(2)
                        if m == 6:
                            known(2)
                            slot_scales(1 - j, i, PER)
                        see(i, j * (SEEN // NOTS) + m)
                    for bt in range(RT):
                        take(R0_NOT + j * RT + bt, 1 - j, bt, U_X + 1 - j, i, R_NOT)
                        for nh in range(2):
                            g = G0_NOT + j * 2 * KT + KT + 2 * bt + nh
                            dve.wait_ge(mm_full, i * G_NOT + (g + 1))
                            V.scalar_tensor_tensor(out=mm[:, g % RING, :], in0=mm[:, g % RING, :],
                                                   scalar=col(u, V_NOT2 + j), in1=bnb[:, nh * HALF:(nh + 1) * HALF],
                                                   op0=ALU.mult, op1=ALU.add).then_inc(biased, 1)
                            see(i, j * (SEEN // NOTS) + KT + 2 * bt + nh)
                    dve.wait_ge(seen_done, i * SEEN + (1 + (j + 1) * (SEEN // NOTS)))
                    step(V.tensor_reduce(col(part_max, X_ALL), piece[:, 0:SEEN // NOTS - 1], AX.X, ALU.max), i, PER)
                    step(V.tensor_tensor(col(part_max, X_ALL), col(part_max, X_ALL), col(field_run, 1), ALU.max), i, PER)
                    step(V.tensor_tensor(col(field_run, 0), col(field_run, 0), col(part_max, X_ALL), ALU.max), i, PER)
            assert steps[0] - base == NOT_STEPS, steps[0] - base
            steps[0] = base + BLOCKS * NOT_STEPS

            step(V.tensor_copy(col(part_max, X_ALL), col(field_run, 0)))
            dve.sem_inc(max_asked, 1)
            dve.wait_ge(max_known, 5 + 3 * NOTS * BLOCKS + 1)
            x_all = col(all_max, X_ALL)
            scale_from(U_ALL, x_all)
            for c, bias, k, pairs_n, s in ((U_RA, X_BA1, 0, AND_PAIRS, S_A1), (U_RO, X_BO1, 1, OR_PAIRS, S_O1)):
                bound = col(rowmax, 0)
                step(V.tensor_reduce(bound, slice_max[:, k * KT:(k + 1) * KT], AX.X, ALU.max))
                step(V.tensor_scalar(bound, bound, x_all, float(2 * H), ALU.mult, ALU.mult))
                step(V.tensor_tensor(bound, bound, col(all_max, bias), ALU.add))
                step(V.tensor_scalar(bound, bound, float(pairs_n), None, ALU.mult))
                scale_from(c, bound)
                step(V.tensor_scalar(b_pair[:, k, :], small[:, s:s + KT], col(up, c), None, ALU.mult))
                step(V.tensor_scalar(u_pair[:, k * KT:(k + 1) * KT], slice_down[:, k * KT:(k + 1) * KT],
                                     col(down, U_ALL), col(up, c), ALU.mult, ALU.mult))
            step(V.tensor_scalar(col(rowmax, 0), x_all, float(F), None, ALU.mult))
            scale_from(U_REM, col(rowmax, 0))
            for dst, a, b in ((V_TOPA, U_RA, U_FA), (V_TOPO, U_RO, U_FO), (V_TOPR, U_REM, U_WT)):
                step(V.tensor_tensor(col(u, dst), col(down, a), col(down, b), ALU.mult))
            dve.sem_inc(scaled, 1)

            for n in range(2 * RT):
                take(R0_AND - 2 * RT + n, n // RT, n % RT, U_ALL)
            with dve.Fori(0, BLOCKS) as i:
                for pair in range(AND_PAIRS):
                    for m in range(KT):
                        g = G0_AND + pair * KT + m
                        if pair == 0:
                            hidden_lo(m, g + 1, i, G_AND)
                        else:
                            t, p0 = tmp[:, m % 2, :], 3 * m
                            dve.wait_ge(act_freed, i * G_AND + (g + 1))
                            V.tensor_tensor(t, t, Hb[:, 0, m, :], ALU.add).then_inc(pair_step, 1)
                            dve.wait_ge(pair_step, i * (3 * KT) + (p0 + 1))
                            V.tensor_tensor(t, t, Hb[:, 1, m, :], ALU.add).then_inc(pair_step, 1)
                            dve.wait_ge(pair_step, i * (3 * KT) + (p0 + 2))
                            V.tensor_copy(Hb[:, 0, m, :], t).then_inc(pair_step, 1)
                            dve.wait_ge(pair_step, i * (3 * KT) + (p0 + 3))
                            V.tensor_tensor(Hb[:, 1, m, :], t, Hb[:, 0, m, :], ALU.subtract).then_inc(h_split, 1)
                        take(R0_AND + pair * 2 * RT + m, 2 * (1 - pair) + m // RT, m % RT, U_ALL, i, R_AND)

            for n in range(2 * RT):
                take(R0_OR - 2 * RT + n, n // RT, n % RT, U_ALL)
            dve.wait_ge(c1_ready, 1)
            with dve.Fori(0, BLOCKS) as i:
                for m in range(KT):
                    hidden_lo(m, G0_OR + m + 1, i, KT)
                    if m % 2:
                        t = m // 2
                        dve.wait_ge(rem_in, i * (16 * RT) + 16 * (t + 1))
                        for j in range(NOTS):
                            dve.wait_ge(rem_t_in[j], i * (16 * RT) + 16 * (t + 1))
                            V.scalar_tensor_tensor(out=rem_sum, in0=rem_t[j], scalar=col(rem_w, F + j), in1=rem_sum,
                                                   op0=ALU.mult, op1=ALU.add).then_inc(rem_step, 1)
                            dve.wait_ge(rem_step, i * (NOTS * RT) + (NOTS * t + j + 1))
                        dve.sem_inc(rem_summed, 1)
                        take(R0_OR + m // 2, 2, m // 2, U_REM, i, R_OR)
                dve.wait_ge(and_in, i * 16 + 16)
                for m in range(MT1):
                    for q, c in enumerate((V_TOPO, V_TOPR)):
                        n = 2 * m + q
                        dve.wait_ge(mm_full, i * G_OR + (G0_OR + KT + n + 1))
                        V.scalar_tensor_tensor(out=acc[:, m, :], in0=mm[:, n % RING, :], scalar=col(u, c),
                                               in1=acc[:, m, :], op0=ALU.mult, op1=ALU.add).then_inc(acc_step, 1)
                        dve.wait_ge(acc_step, i * (3 * MT1) + (3 * m + q + 1))
                        dve.sem_inc(dve_freed, 1)
                    dve.wait_ge(tl_full, i * T_OR + (1 + m + 1))
                    V.scalar_tensor_tensor(out=acc[:, m, :], in0=acc[:, m, :], scalar=invc[:, 0:1],
                                           in1=tl[:, m % 2, :], op0=ALU.mult, op1=ALU.add).then_inc(acc_step, 1)
                    dve.wait_ge(acc_step, i * (3 * MT1) + (3 * m + 3))
                    dve.sem_inc(tl_freed, 1)
                    for n in (2 * m, 2 * m + 1):
                        take(R0_OR + RT + n, n // RT, n % RT, U_ALL, i, R_OR)


def weight_slices(w):
    k, m = w.shape
    return np.ascontiguousarray(w.reshape(k // P, P, m // P, P).transpose(2, 1, 0, 3)).reshape(m // P, P, k)


def by_partition(w):
    k, n = w.shape
    return np.ascontiguousarray(w.reshape(k // P, P, n).transpose(1, 0, 2)).reshape(P, k // P * n)


def kernel(**inputs):
    import concourse.bacc as bacc
    from concourse.bass_utils import run_bass_kernel_spmd

    a = {k: np.asarray(v) for k, v in inputs.items()}
    consts = np.zeros((P, K_COLS), np.float32)
    consts[:, K_FIELD:K_FIELD + F] = np.arange(F)
    consts[:, K_START:K_START + F] = TABLE_START
    consts[:, K_LAST:K_LAST + F] = [n - 1 for n in TABLE_ROWS]
    consts[:, K_ROW:K_ROW + TILES] = np.arange(B).reshape(TILES, P).T
    consts[:, K_IDENT:] = np.eye(P)
    w_top1, w_z = a["W_top1"], a["W_top1"][:H]
    names = ["L0_rec_bn1", "L0_rec_ba1", "L0_rec_bo1", "L0_rec_ba2", "L0_rec_bo2", "b_top1", "b_top2"]
    smalls = [a[n].reshape(-1, P).T for n in names] + [a["W_top3"].reshape(MT2, P).T]
    n1 = weight_slices(a["L0_rec_Wn1"])
    data = {
        "table": np.concatenate([a[f"tbl_{f}"] for f in range(F)], axis=0),
        "ids": np.ascontiguousarray(a["ids"].reshape(TILES, P, F).transpose(1, 0, 2)).reshape(P, TILES * F),
        "fields": np.concatenate([a["L0_rec_not_idx"].reshape(-1), a["L0_rec_and_pairs"].reshape(-1),
                                  a["L0_rec_or_pairs"].reshape(-1)]),
        "consts": consts,
        "smalls": np.ascontiguousarray(np.concatenate(smalls, axis=1)),
        "bn2": a["L0_rec_bn2"],
        "wn1": np.ascontiguousarray(n1.transpose(1, 0, 2)).reshape(P, KT * H),
        "wn2": by_partition(a["L0_rec_Wn2"]),
        "pair_w": np.concatenate([weight_slices(a["L0_rec_Wa1"]), weight_slices(a["L0_rec_Wo1"])]),
        "w2ta": weight_slices(a["L0_rec_Wa2"].T),
        "w2to": weight_slices(a["L0_rec_Wo2"].T),
        "wt1": by_partition(w_z),
        "wt1d": np.ascontiguousarray(w_top1[H:]),
        "wt2": by_partition(a["W_top2"]),
        "dense_t": np.ascontiguousarray(a["dense_ctx"].T),
    }
    nc = bacc.Bacc("TRN2", target_bir_lowering=False, num_devices=1)
    args = {k: nc.dram_tensor(f"in_{k}", v.shape, mybir.dt.from_np(v.dtype), kind="ExternalInput").ap()
            for k, v in data.items()}
    y = nc.dram_tensor("y", (B, 1), mybir.dt.float32, kind="ExternalOutput").ap()
    build(nc, **args, out=y)
    r = run_bass_kernel_spmd(nc, [{f"in_{k}": v for k, v in data.items()}], core_ids=[0])
    return r.results[0]["y"]
```

```python
from contextlib import ExitStack

import numpy as np

import concourse.bass as bass
from concourse import mybir

B, F, H = 2048, 8, 1024
D, M1, M2 = 16, 512, 256
TABLE_ROWS = [1250, 1000, 1250, 12500, 1000, 1250, 12500, 1250]
TABLE_START = [sum(TABLE_ROWS[:f]) for f in range(F)]
ALL_ROWS = sum(TABLE_ROWS)
NOTS, AND_PAIRS, OR_PAIRS = 2, 2, 1
P = 128
KT = H // P
MT1, MT2 = M1 // P, M2 // P
BLOCK = 512
BLOCKS = B // BLOCK
RT = BLOCK // P
TILES = B // P
HALF = H // 2

SLOTS = 2 * (AND_PAIRS + OR_PAIRS)
C_NOT = 0
C_PX = C_NOT + NOTS
C_PT = C_PX + SLOTS
C_ALL = C_PT + SLOTS
COLS = C_ALL + F
SKIP = 1 << 20

K_FIELD, K_START, K_LAST, K_ROW, K_IDENT = 0, F, 2 * F, 3 * F, 3 * F + TILES
K_COLS = K_IDENT + P
S_N1, S_A1, S_O1, S_A2, S_O2 = 0, KT, 2 * KT, 3 * KT, 4 * KT
S_T1 = 5 * KT
S_T2 = S_T1 + MT1
S_W3 = S_T2 + MT2
S_COLS = S_W3 + MT2

RING = 4
G_FOLD = 2 * KT
G_NOT = NOTS * 2 * KT
G_AND = AND_PAIRS * KT + MT1
G_OR = KT + 2 * MT1
G0_NOT = G_FOLD
G0_AND = G0_NOT + BLOCKS * G_NOT
G0_OR = G0_AND + BLOCKS * G_AND
R_NOT, R_AND, R_OR = NOTS * RT, 2 * AND_PAIRS * RT, 3 * RT
R0_NOT = RT
R0_AND = R0_NOT + BLOCKS * R_NOT + 2 * RT
R0_OR = R0_AND + BLOCKS * R_AND
T_OR = MT1 + MT2 + 1
T_STORES = 16 * (1 + BLOCKS * NOTS * RT // 2)
R_STORES = 16 * (1 + BLOCKS * RT // 2)
SEEN = F * RT
SEEN_FIRST = 5
SPLIT_NOT = 1 + BLOCKS * NOTS * KT
SPLIT_AND = SPLIT_NOT + BLOCKS * AND_PAIRS * KT
PAIR_SLICES, SLICE = 2 * KT, 2 * H
IN_N2, IN_FA, IN_FO, IN_WT = KT, 2 * KT, 2 * KT + KT // 2, 3 * KT
X_BN1, X_BA1, X_BO1, X_N1, X_N2, X_FA, X_FO, X_WT, X_ROW, X_JOB, X_ALL = 0, 1, 2, 3, 4, 5, 6, 7, 8, 10, 12
U_N1, U_N2, U_FA, U_FO, U_WT, U_X, U_H, U_ALL, U_RA, U_RO, U_REM, U_JOB = 0, 1, 2, 3, 4, 5, 7, 9, 10, 11, 12, 13
V_NOT1, V_NOT2, V_TOPA, V_TOPO, V_TOPR, V_BOUND = 0, 2, 4, 5, 6, 7
EXPONENT = 0x7F800000
LEAST = 2.0 ** -46
NOT_STEPS = NOTS * 34


def build(nc, table, ids, fields, consts, smalls, bn2, wn1, wn2, pair_w, w2ta, w2to, wt1, wt1d,
          wt2, dense_t, out):
    fp32, fp16, i32 = mybir.dt.float32, mybir.dt.float16, mybir.dt.int32
    ALU, ACT, AX = mybir.AluOpType, mybir.ActivationFunctionType, mybir.AxisListType
    MAX = bass.bass_isa.ReduceOp.max

    ctx = ExitStack()
    with ctx:
        def sb(name, shape, dt=fp32):
            return ctx.enter_context(nc.sbuf_tensor(name, shape, dt))

        def sem(name):
            return ctx.enter_context(nc.semaphore(name))

        def dram(name, shape, dt=fp32):
            return nc.dram_tensor(name, shape, dt, kind="Internal").ap()

        t_rows = dram("t_rows", (NOTS * B, H))
        and_dram = dram("and_dram", (BLOCKS * P, MT1 * BLOCK))
        pair_split = dram("pair_split", (PAIR_SLICES, P, 2 * SLICE), fp16)
        fo_split = dram("fo_split", (P, 2 * KT * M1), fp16)
        wt_split = dram("wt_split", (P, 2 * KT * M1), fp16)
        rem_rows = dram("rem_rows", (B, H))
        token = dram("token", (7, P))

        W = sb("W", [P, 16 * 2 * H], fp16)
        X = sb("X", [P, 4, 2, KT, BLOCK], fp16)
        Hb = sb("Hb", [P, 2, KT, BLOCK], fp16)
        Fw = sb("Fw", [P, 2 * KT * M1], fp16)
        Wt = sb("Wt", [P, 2 * KT * M1], fp16)
        rows = sb("rows", [P, 2, H])
        acc = sb("acc", [P, MT1, BLOCK])
        tmp = sb("tmp", [P, 2, BLOCK])
        side = sb("side", [P, 2, BLOCK])
        cst = sb("cst", [P, K_COLS])
        small = sb("small", [P, S_COLS])
        bvec = sb("bvec", [P, KT])
        c1 = sb("c1", [P, MT1])
        invc = sb("invc", [P, 1])
        rem_w = sb("rem_w", [P, F + NOTS])
        idx = sb("idx", [P, TILES + RT, COLS], i32)
        stage = sb("stage", [P, 2, RT, COLS], i32)
        part_max = sb("part_max", [P, 16])
        all_max = sb("all_max", [P, 16])
        piece = sb("piece", [P, 16])
        up = sb("up", [P, 16])
        down = sb("down", [P, 16])
        u = sb("u", [P, 16])
        rowmax = sb("rowmax", [P, 8])
        slice_max = sb("slice_max", [P, PAIR_SLICES])
        slice_down = sb("slice_down", [P, PAIR_SLICES])
        u_pair = sb("u_pair", [P, PAIR_SLICES])
        b_not = sb("b_not", [P, NOTS, KT])
        b_pair = sb("b_pair", [P, 2, KT])
        field_run = sb("field_run", [P, 2])

        ident = cst[:, K_IDENT:K_IDENT + P]
        W_not = W[:, :].rearrange("p (s h n) -> p s h n", s=16, h=2)
        W_pair = W[:, :].rearrange("p (s h n) -> p s h n", s=KT, h=2)
        Fs = Fw[:, :].rearrange("p (s h n) -> p s h n", s=KT // 2, h=2)
        Ts = Wt[:, :].rearrange("p (s h n) -> p s h n", s=KT // 2, h=2)
        F32 = Fw[:, :].bitcast(fp32).rearrange("p (k n) -> p k n", k=KT)
        T32 = Wt[:, :].bitcast(fp32).rearrange("p (k n) -> p k n", k=KT)

        def as_rows(slot):
            return X[:, slot, :, :, :].rearrange("p h k n -> p (h k n)").bitcast(fp32)

        scr = as_rows(0)
        fold_w = as_rows(1).rearrange("p (s k m) -> p s k m", s=RING, k=KT)
        not_rows = as_rows(2).rearrange("p (s n) -> p s n", n=H)
        first_rows = [as_rows(3 - n // RT)[:, n % RT * H:(n % RT + 1) * H] for n in range(2 * RT)]
        job_in_f = as_rows(3)[:, 0:SLICE]
        job_out = as_rows(3)[:, SLICE:2 * SLICE].bitcast(fp16).rearrange("p (h n) -> p h n", h=2)
        Fo32 = as_rows(3).rearrange("p (k n) -> p k n", k=KT)
        Fos = X[:, 3, :, :, :].rearrange("p h k n -> p (h k n)").rearrange("p (s h n) -> p s h n", s=KT // 2, h=2)
        rem_area = as_rows(3).rearrange("p (s n) -> p s n", n=H)
        rem_sum, rem_t = rem_area[:, 0, :], [rem_area[:, 1 + j, :] for j in range(NOTS)]
        rem_acc = Wt[:, :].bitcast(fp32).rearrange("p (s n) -> p s n", n=H)
        wt2s = rem_area[:, 3, :].rearrange("p (k n) -> p k n", k=MT1)
        t_out = acc[:, :, :].rearrange("p m n -> p (m n)").rearrange("p (s n) -> p s n", n=H)
        bnb = rows[:, 0, :]
        side_row = side[:, :, :].rearrange("p a n -> p (a n)")
        seen = [rows[:, 1, :], side_row]
        copied = [rows[:, 1, :], side_row]
        wt1ds, dens = side[0:D, 0, :], side[0:D, 1, :]

        mm = ctx.enter_context(nc.psum_tensor("mm", [P, RING, BLOCK], fp32))
        tp = ctx.enter_context(nc.psum_tensor("tp", [P, 2, BLOCK], fp32))
        tl = ctx.enter_context(nc.psum_tensor("tl", [P, 2, BLOCK], fp32))

        consts_in, smalls_in, ints_in = sem("consts_in"), sem("smalls_in"), sem("ints_in")
        bn2_in, wt_in = sem("bn2_in"), sem("wt_in")
        fold_in = [sem(f"fold_in{s}") for s in range(RING)]
        fo_out, fo_in = sem("fo_out"), sem("fo_in")
        wn1_in, wn2_in = sem("wn1_in"), sem("wn2_in")
        slice_in = [sem(f"slice_in{m}") for m in range(KT)]
        job_read, job_stored = sem("job_read"), sem("job_stored")
        top_in, dense_in, and_in, and_out = sem("top_in"), sem("dense_in"), sem("and_in"), sem("and_out")
        t_stored = [sem(f"t_stored{s}") for s in range(2)]
        y_out = sem("y_out")
        dve_step = sem("dve_step")
        idx_ready, bvec_ready = sem("idx_ready"), sem("bvec_ready")
        staged, pool_holds = sem("staged"), sem("pool_holds")
        sp_holds = sem("sp_holds")
        max_asked, max_known = sem("max_asked"), sem("max_known")
        scaled = sem("scaled")
        slot_scaled = sem("slot_scaled")
        job_scaled = sem("job_scaled")
        copy_done, hi_done, lo_done = sem("copy_done"), sem("hi_done"), sem("lo_done")
        job_hi, job_lo = sem("job_hi"), sem("job_lo")
        not_in = [sem(f"not_in{s}") for s in range(RT)]
        seen_in = [sem(f"seen_in{s}") for s in range(2)]
        seen_done = sem("seen_done")
        x_in = [sem(f"x_in{s}") for s in range(2)]
        row_in = [sem(f"row_in{s}") for s in range(2)]
        first_in = [sem(f"first_in{n}") for n in range(2 * RT)]
        wt_out, wt_back = sem("wt_out"), sem("wt_back")
        rem_stored = [sem(f"rem_stored{s}") for s in range(2)]
        rem_in, rem_t_in = sem("rem_in"), [sem(f"rem_t_in{j}") for j in range(NOTS)]
        rem_step, rem_summed = sem("rem_step"), sem("rem_summed")
        mm_full = sem("mm_full")
        act_freed = sem("act_freed")
        dve_freed = sem("dve_freed")
        biased = sem("biased")
        h_split = sem("h_split")
        pair_step = sem("pair_step")
        turned = [sem("turned_a"), sem("turned_b")]
        high = [sem("high_a"), sem("high_b")]
        taken = [sem("taken_a"), sem("taken_b")]
        tl_full, tl_freed = sem("tl_full"), sem("tl_freed")
        h1_ready = sem("h1_ready")
        c1_ready, y_ready = sem("c1_ready"), sem("y_ready")
        acc_step = sem("acc_step")

        block = ctx.enter_context(nc.Block())

        @block.sync
        def _(sp):
            sp.dma_start(cst[:, :], consts).then_inc(consts_in, 16)
            sp.dma_start(scr[:, 0:TILES * F].bitcast(i32), ids).then_inc(ints_in, 16)
            sp.dma_start(scr[:, TILES * F:TILES * F + F].bitcast(i32),
                         fields.partition_broadcast(P)).then_inc(ints_in, 16)
            sp.dma_start(small[:, :], smalls).then_inc(smalls_in, 16)
            sp.dma_start(T32, wt1.rearrange("p (k n) -> p k n", k=KT)).then_inc(wt_in, 16)
            for n in range(G_FOLD):
                if n >= RING:
                    sp.wait_ge(mm_full, n - RING + 1)
                w = w2ta if n < KT else w2to
                sp.dma_start(fold_w[:, n % RING, :, :].rearrange("p k m -> p (k m)"), w[n % KT]).then_inc(fold_in[n % RING], 16)
                if n == 1:
                    sp.dma_start(W[:, 0:KT * 2 * H].bitcast(fp32), wn1).then_inc(wn1_in, 16)
                if n == RING:
                    sp.dma_start(W[:, KT * 2 * H:2 * KT * 2 * H].bitcast(fp32), wn2).then_inc(wn2_in, 16)
                    sp.dma_start(bnb, bn2.partition_broadcast(P)).then_inc(bn2_in, 16)
                    for q, s in enumerate(t_stored + [and_out, y_out, job_stored] + rem_stored):
                        sp.dma_start(token[q:q + 1, :], consts[0:1, 0:P]).then_inc(s, 16)
            sp.wait_ge(lo_done, IN_FO + KT // 2)
            sp.dma_start(fo_split, X[:, 3, :, :, :].rearrange("p h k n -> p (h k n)")).then_inc(fo_out, 16)
            sp.wait_ge(fo_out, 16)
            sp.wait_ge(lo_done, IN_WT + KT // 2)
            sp.dma_start(wt_split, Wt[:, :]).then_inc(wt_out, 16)
            def job_load(i, c):
                sp.wait_ge(job_lo, i * 4 + (c + 1))
                sp.dma_start(job_in_f, pair_w[bass.ds(i * 4 + c, 1), :, :].rearrange("a p n -> (a p) n")).then_inc(job_read, 16)

            def job_store(i, c):
                sp.wait_ge(job_lo, i * 4 + (c + 2))
                sp.dma_start(pair_split[bass.ds(i * 4 + c, 1), :, :].rearrange("a p n -> (a p) n"),
                             job_out.rearrange("p h n -> p (h n)")).then_inc(job_stored, 16)

            def rem_store(i, t):
                sp.wait_ge(seen_done, i * SEEN + (1 + (t + 1) * F))
                sp.dma_start(rem_rows[bass.ds(i * BLOCK + t * P, P), :], rem_acc[:, t % 2, :]).then_inc(rem_stored[t % 2], 16)

            with sp.Fori(0, BLOCKS) as i:
                for j in range(NOTS):
                    job_load(i, 2 * j)
                    job_store(i, 2 * j)
                    job_load(i, 2 * j + 1)
                    for bt in range(RT):
                        if bt == 1:
                            rem_store(i, 2 * j)
                        if bt == 2:
                            job_store(i, 2 * j + 1)
                        g = G0_NOT + j * 2 * KT + KT + 2 * bt + 1
                        sp.wait_ge(act_freed, i * G_NOT + (g + 1))
                        sp.dma_start(t_rows[bass.ds(i * BLOCK + (j * B + bt * P), P), :],
                                     t_out[:, bt % 2, :]).then_inc(t_stored[bt % 2], 16)
                    rem_store(i, 2 * j + 1)
            sp.wait_ge(job_stored, 16 * (1 + PAIR_SLICES))

            def pair_slice(m, q):
                sp.dma_start(W_pair[:, m, :, :].rearrange("p h n -> p (h n)"), pair_split[q]).then_inc(slice_in[m], 16)

            for m in range(KT):
                if m == 2:
                    for n in range(2 * RT):
                        sp.wait_ge(first_in[n], 32)
                sp.wait_ge(mm_full, (G0_NOT + (BLOCKS - 1) * G_NOT + 2 * KT + 2 * m + 2) if m < KT // 2 else G0_AND)
                pair_slice(m, m)
            sp.wait_ge(wt_out, 16)
            for s in range(2):
                sp.wait_ge(t_stored[s], T_STORES)
                sp.wait_ge(rem_stored[s], R_STORES)
            sp.dma_start(Wt[:, :], wt_split).then_inc(wt_back, 16)
            for m in range(KT):
                sp.wait_ge(mm_full, G0_AND + (BLOCKS - 1) * G_AND + KT + m + 1)
                pair_slice(m, KT + m)
            sp.wait_ge(mm_full, G0_OR - MT1)
            def rem_load(i, t):
                sp.wait_ge(turned[1], i * R_OR + (R0_OR - 2 * RT if t == 0 else R0_OR + t))
                sp.dma_start(rem_sum, rem_rows[bass.ds(i * BLOCK + t * P, P), :]).then_inc(rem_in, 16)
                sp.wait_ge(rem_summed, i * RT + (t + 1))
                for j in range(NOTS):
                    sp.dma_start(rem_t[j], t_rows[bass.ds(i * BLOCK + (j * B + t * P), P), :]).then_inc(rem_t_in[j], 16)

            with sp.Fori(0, BLOCKS) as i:
                rem_load(i, 0)
                sp.wait_ge(and_out, 16 * (1 + BLOCKS))
                sp.wait_ge(tl_full, i * T_OR + 1)
                sp.wait_ge(y_out, i * 16 + 16)
                sp.sem_inc(sp_holds, 1)
                sp.dma_start(dens, dense_t[:, bass.ds(i * BLOCK, BLOCK)]).then_inc(dense_in, 16)
                sp.dma_start(acc[:, :, :].rearrange("p m n -> p (m n)"), and_dram[bass.ds(i * P, P), :]).then_inc(and_in, 16)
                for t in range(1, RT):
                    rem_load(i, t)
                sp.wait_ge(y_ready, i + 2)
                sp.dma_start(out.rearrange("b o -> o b")[:, bass.ds(i * BLOCK, BLOCK)], acc[0:1, 0, :]).then_inc(y_out, 16)
            sp.wait_ge(y_out, 16 * (1 + BLOCKS))

        @block.gpsimd
        def _(pool):
            def hold(what, value):
                pool.wait_ge(what, value)
                pool.sem_inc(pool_holds, 1)

            def gather(dst, source, bound, index):
                return pool.indirect_dma_start(dst, None, source, bass.IndirectOffsetOnAxis(ap=index, axis=0),
                                               bounds_check=bound, oob_is_err=False)

            def pair_row(tile, slot, buf, n, i=None, per=0):
                gather(rows[:, buf, :], table, ALL_ROWS - 1,
                       stage[:, tile // RT, tile % RT, C_PX + slot:C_PX + slot + 1]).then_inc(x_in[buf], 16)
                hold(x_in[buf], 16 * (n + 1) if i is None else i * per + 16 * (n + 1))
                gather(rows[:, buf, :], t_rows, NOTS * B - 1,
                       stage[:, tile // RT, tile % RT, C_PT + slot:C_PT + slot + 1]).then_inc(row_in[buf], 16)

            def over_partitions(c, n, asked, i=None, per=0):
                hold(max_asked, asked if i is None else i * per + asked)
                pool.partition_all_reduce(all_max[:, c:c + n], part_max[:, c:c + n], channels=P,
                                          reduce_op=MAX).then_inc(max_known, 1)

            hold(idx_ready, 1)
            for t in range(RT):
                gather(not_rows[:, t, :], table, ALL_ROWS - 1, idx[:, t, C_NOT:C_NOT + 1]).then_inc(not_in[t], 16)
            over_partitions(X_BN1, 4, 1)
            over_partitions(X_N2, 1, 2)
            over_partitions(X_ROW, 1, 3)
            over_partitions(X_FA, 1, 4)
            over_partitions(X_FO, 2, 5)
            with pool.Fori(0, BLOCKS) as i:
                for t in range(RT):
                    hold(not_in[t], i * (16 * NOTS) + 16)
                hold(seen_done, i * SEEN + 1)
                pool.tensor_copy(stage[:, 0, :, :], idx[:, bass.ds(i * RT, RT), :]).then_inc(staged, 1)
                pool.tensor_copy(stage[:, 1, :, :], idx[:, bass.ds(i * RT + RT, RT), :]).then_inc(staged, 1)
                hold(staged, i * 2 + 2)
                for j in range(NOTS):
                    asked = 5 + 3 * j
                    if j == 0:
                        hold(lo_done, IN_WT + KT // 2)
                    for k in range(SEEN // NOTS):
                        if k == 2:
                            for t in range(RT):
                                hold(turned[1], i * R_NOT + (j * RT + t + 1))
                                gather(not_rows[:, t, :], table, ALL_ROWS - 1,
                                       stage[:, j, t, C_NOT + 1 - j:C_NOT + 2 - j]).then_inc(not_in[t], 16)
                        for q, (at, c) in enumerate(((4, X_JOB), (7, X_ROW + 1 - j), (8, X_JOB + 1))):
                            if k == at:
                                over_partitions(c, 1, asked + q + 1, i, 3 * NOTS)
                        n = j * (SEEN // NOTS) + k
                        t, f = n // F, n % F
                        if n < 2:
                            hold(seen_done, i * SEEN + 1)
                        else:
                            hold(seen_done, i * SEEN + n)
                        gather(seen[n % 2], table, ALL_ROWS - 1,
                               stage[:, 0, t, C_ALL + f:C_ALL + f + 1]).then_inc(seen_in[n % 2], 16)
            hold(job_stored, 16 * (1 + PAIR_SLICES))
            def first_table(n):
                if n >= RT:
                    hold(turned[1], R0_AND - 4 * RT + n + 1)
                gather(first_rows[n], table, ALL_ROWS - 1,
                       idx[:, n % RT, C_PX + n // RT:C_PX + n // RT + 1]).then_inc(first_in[n], 16)

            for n in range(RT):
                first_table(n)
            over_partitions(X_ALL, 1, 5 + 3 * NOTS * BLOCKS + 1)
            for s in range(2):
                hold(t_stored[s], T_STORES)
            for n in range(2 * RT):
                hold(first_in[n], 16)
                gather(first_rows[n], t_rows, NOTS * B - 1,
                       idx[:, n % RT, C_PT + n // RT:C_PT + n // RT + 1]).then_inc(first_in[n], 16)
                if n < RT:
                    first_table(RT + n)
            with pool.Fori(0, BLOCKS) as i:
                hold(turned[1], i * R_AND + R0_AND)
                pool.tensor_copy(stage[:, 0, :, :], idx[:, bass.ds(i * RT, RT), :]).then_inc(staged, 1)
                pool.tensor_copy(stage[:, 1, :, :], idx[:, bass.ds(i * RT + RT, RT), :]).then_inc(staged, 1)
                hold(staged, i * 2 + (2 * BLOCKS + 2))
                for n in range(R_AND):
                    hold(turned[1], i * R_AND + (R0_AND + n - 1))
                    pair = 1 - n // (2 * RT)
                    pair_row((1 - pair) * RT + n % RT, 2 * pair + n // RT % 2, n % 2,
                             n // 2, i, 16 * R_AND // 2)
            used = BLOCKS * R_AND // 2
            with pool.Fori(0, BLOCKS) as i:
                for s in range(2):
                    hold(row_in[s], i * (16 * RT) + 16 * used)
                pool.tensor_copy(stage[:, 0, :, :], idx[:, bass.ds(i * RT, RT), :]).then_inc(staged, 1)
                pool.tensor_copy(stage[:, 1, :, :], idx[:, bass.ds(i * RT + RT, RT), :]).then_inc(staged, 1)
                hold(staged, i * 2 + (4 * BLOCKS + 2))
                for n in range(2 * RT):
                    hold(turned[1], i * R_OR + (R0_OR + (RT if n > 1 else 0) + n - 1))
                    pair_row(RT + n % RT, 2 * AND_PAIRS + n // RT, n % 2, used + n // 2, i, 16 * RT)

        @block.tensor
        def _(pe):
            pe.wait_ge(consts_in, 16)
            pe.wait_ge(wt_in, 16)

            def turn(src, r, i=None, per=0):
                for h in range(2):
                    if i is not None or r:
                        pe.wait_ge(taken[h], r if i is None else i * per + r)
                    for k in range(KT // 2):
                        kk = h * (KT // 2) + k
                        last = pe.transpose(tp[:, h, k * P:(k + 1) * P], src[:, kk * P:(kk + 1) * P], ident)
                    last.then_inc(turned[h], 1)

            def products(bank, pairs, second_half=None):
                n = 0
                for q, (a, b) in enumerate(pairs):
                    if second_half and q == len(pairs) // 2:
                        second_half()
                    for pa, pb in ((0, 0), (0, 1), (1, 0)):
                        last = pe.matmul(bank, a(pa), b(pb), start=(n == 0), stop=(n == 3 * len(pairs) - 1))
                        n += 1
                return last

            for n in range(G_FOLD):
                pe.wait_ge(fold_in[n % RING], 16 * (n // RING + 1))
                if n >= RING:
                    pe.wait_ge(act_freed, n - RING + 1)
                for k in range(KT):
                    last = pe.matmul(mm[:, n % RING, :], fold_w[:, n % RING, k, :], T32[:, k, :],
                                     start=(k == 0), stop=(k == KT - 1))
                last.then_inc(mm_full, 1)
            pe.wait_ge(bvec_ready, 1)
            for m in range(MT1):
                for k in range(KT):
                    last = pe.matmul(tl[:, 0, m:m + 1], T32[:, k, m * P:(m + 1) * P], bvec[:, k:k + 1],
                                     start=(k == 0), stop=(k == KT - 1))
                if m == MT1 - 1:
                    last.then_inc(tl_full, 1)
                if m < RT:
                    pe.wait_ge(not_in[m], 16)
                    turn(not_rows[:, m, :], m)

            with pe.Fori(0, BLOCKS) as i:
                for j in range(NOTS):
                    for h in range(2):
                        pe.wait_ge(taken[h], i * R_NOT + (R0_NOT + j * RT))
                    if j == 0:
                        pe.wait_ge(lo_done, IN_N2)
                    for m in range(KT):
                        g = G0_NOT + j * 2 * KT + m
                        pe.wait_ge(act_freed, i * G_NOT + (g - RING + 1))
                        products(mm[:, g % RING, :],
                                 [(lambda h, k=k: W_not[:, m, h, k * P:(k + 1) * P],
                                   lambda h, k=k: X[:, j, h, k, :]) for k in range(KT)]).then_inc(mm_full, 1)
                    if j == 0:
                        pe.wait_ge(lo_done, IN_N2 + KT)
                    for bt in range(RT):
                        pe.wait_ge(not_in[bt], i * (16 * NOTS) + 16 * (j + 2))
                        turn(not_rows[:, bt, :], R0_NOT + j * RT + bt, i, R_NOT)
                        if bt == 0:
                            pe.wait_ge(h_split, i * (NOTS * KT) + (j * KT + KT + 1))
                        for nh in range(2):
                            g = G0_NOT + j * 2 * KT + KT + 2 * bt + nh
                            pe.wait_ge(act_freed, i * G_NOT + (g - RING + 1))
                            products(mm[:, g % RING, :],
                                     [(lambda h, k=k: Hb[:, h, k, bt * P:(bt + 1) * P],
                                       lambda h, k=k: W_not[:, KT + k, h, nh * HALF:(nh + 1) * HALF])
                                      for k in range(KT)]).then_inc(mm_full, 1)

            def pair_group(bank, m, s0, second_half=None):
                return products(mm[:, bank, :],
                                [(lambda h, k=k: W_pair[:, m, h, k * P:(k + 1) * P],
                                  lambda h, k=k: X[:, s0 + k // KT, h, k % KT, :]) for k in range(2 * KT)],
                                second_half)

            def top_group(bank, m, weights, x):
                return products(mm[:, bank, :],
                                [(lambda h, k=k: weights[:, k // 2, h, (k % 2) * M1 + m * P:(k % 2) * M1 + (m + 1) * P],
                                  lambda h, k=k: x[:, h, k, :]) for k in range(KT)])

            for n in range(2 * RT):
                pe.wait_ge(first_in[n], 32)
                turn(first_rows[n], R0_AND - 2 * RT + n)
            with pe.Fori(0, BLOCKS) as i:
                for pair in range(AND_PAIRS):
                    def vectors_whole():
                        for h in range(2):
                            pe.wait_ge(taken[h], i * R_AND + (R0_AND + pair * 2 * RT))

                    for m in range(KT):
                        g = G0_AND + pair * KT + m
                        pe.wait_ge(slice_in[m], 16)
                        pe.wait_ge(act_freed, i * G_AND + (g - RING + 1))
                        pair_group(g % RING, m, 2 * pair, None if m else vectors_whole).then_inc(mm_full, 1)
                        n = pair * 2 * RT + m
                        pe.wait_ge(row_in[n % 2], i * (16 * R_AND // 2) + 16 * (n // 2 + 1))
                        turn(rows[:, n % 2, :], R0_AND + n, i, R_AND)
                pe.wait_ge(h_split, i * (2 * KT) + (SPLIT_NOT + 2 * KT))
                for m in range(MT1):
                    g = G0_AND + AND_PAIRS * KT + m
                    pe.wait_ge(act_freed, i * G_AND + (g - RING + 1))
                    top_group(g % RING, m, Fs, Hb).then_inc(mm_full, 1)

            used = BLOCKS * R_AND // 2
            pe.wait_ge(act_freed, G0_OR)
            with pe.Fori(0, BLOCKS) as i:
                def vectors_whole():
                    for h in range(2):
                        pe.wait_ge(taken[h], i * R_OR + R0_OR)

                for m in range(KT):
                    pe.wait_ge(slice_in[m], 32)
                    if m < RING:
                        pe.wait_ge(dve_freed, i * (2 * MT1) + (MT1 + m + 1))
                    else:
                        pe.wait_ge(act_freed, i * KT + (G0_OR + m - RING + 1))
                    pair_group(m % RING, m, 0, None if m else vectors_whole).then_inc(mm_full, 1)
                    if m % 2:
                        pe.wait_ge(rem_summed, i * RT + (m // 2 + 2))
                        turn(rem_sum, R0_OR + m // 2, i, R_OR)
                for h in range(2):
                    pe.wait_ge(taken[h], i * R_OR + (R0_OR + RT))
                pe.wait_ge(dense_in, i * 16 + 16)
                pe.wait_ge(top_in, 32)
                pe.wait_ge(fo_in, 16)
                pe.wait_ge(wt_back, 16)
                for m in range(MT1):
                    for q, (weights, x) in enumerate(((Ts, X[:, 2, :, :, :]), (Fs, Hb))):
                        n = 2 * m + q
                        if n == 1:
                            pe.wait_ge(h_split, i * KT + (SPLIT_AND + KT))
                        if n < RING:
                            pe.wait_ge(act_freed, i * KT + (G0_OR + KT - RING + n + 1))
                        else:
                            pe.wait_ge(dve_freed, i * (2 * MT1) + (2 * MT1 + n - RING + 1))
                        top_group(n % RING, m, weights, x).then_inc(mm_full, 1)
                        if q:
                            pe.wait_ge(tl_freed, i * T_OR + max(m, 1))
                            pe.matmul(tl[:, m % 2, :], wt1ds[:, m * P:(m + 1) * P], dens,
                                      start=True, stop=True).then_inc(tl_full, 1)
                        pe.wait_ge(row_in[n % 2], i * (16 * RT) + 16 * (used + n // 2 + 1))
                        turn(rows[:, n % 2, :], R0_OR + RT + n, i, R_OR)
                pe.wait_ge(h1_ready, i * MT1 + MT1)
                for m in range(MT2):
                    pe.wait_ge(tl_freed, i * T_OR + (MT1 + m))
                    for k in range(MT1):
                        last = pe.matmul(tl[:, m % 2, :], wt2s[:, k, m * P:(m + 1) * P], acc[:, k, :],
                                         start=(k == 0), stop=(k == MT1 - 1))
                    last.then_inc(tl_full, 1)
                pe.wait_ge(tl_freed, i * T_OR + (MT1 + MT2 + 1))
                for k in range(MT2):
                    last = pe.matmul(tl[0:1, 0, :], small[:, S_W3 + k:S_W3 + k + 1], tmp[:, k, :],
                                     start=(k == 0), stop=(k == MT2 - 1))
                last.then_inc(tl_full, 1)

        @block.scalar
        def _(act):
            A = nc.scalar.activation

            def take(r, slot, t, scale, i=None, per=0):
                for h in range(2):
                    act.wait_ge(turned[h], (r if i is None else i * per + r) + 1)
                    A(X[:, slot, 0, h * KT // 2:(h + 1) * KT // 2, t * P:(t + 1) * P],
                      tp[:, h, :].rearrange("p (k b) -> p k b", k=KT // 2),
                      ACT.Copy, scale=up[:, scale:scale + 1]).then_inc(high[h], 1)

            def fold_out(n):
                act.wait_ge(mm_full, n + 1)
                dst = F32[:, n, :] if n < KT else Fo32[:, n - KT, :]
                A(dst, mm[:, n % RING, :], ACT.Copy).then_inc(act_freed, 1)

            def split_in_place(n, hi, whole, scale, ready):
                act.wait_ge(scaled, ready)
                if n >= 2:
                    act.wait_ge(lo_done, n - 1)
                A(copied[n % 2], whole, ACT.Copy).then_inc(copy_done, 1)
                act.wait_ge(copy_done, n + 1)
                A(hi, copied[n % 2], ACT.Copy, scale=up[:, scale:scale + 1]).then_inc(hi_done, 1)

            def slice_of(n):
                if n < IN_FA:
                    return W_not[:, n, 0, :], W_not[:, n, :, :].rearrange("p h n -> p (h n)").bitcast(fp32), \
                        (U_N1 if n < KT else U_N2), (1 if n < KT else 2)
                src, c, base, ready = ((Fs, U_FA, IN_FA, 3) if n < IN_FO else
                                       (Fos, U_FO, IN_FO, 5) if n < IN_WT else (Ts, U_WT, IN_WT, 5))
                v = src[:, n - base, :, :]
                return v[:, 0, :], v.rearrange("p h n -> p (h n)").bitcast(fp32), c, ready

            def split(n):
                hi, whole, scale, ready = slice_of(n)
                split_in_place(n, hi, whole, scale, ready)

            for n in range(RING):
                fold_out(n)
            for n in range(KT):
                split(2 * n)
                split(2 * n + 1)
                fold_out(RING + n)
            for n in range(RING):
                split(IN_FA + n)
                fold_out(RING + KT + n)
            act.wait_ge(slot_scaled, 1)
            for t in range(RT):
                take(t, 0, t, U_X)
                split(IN_FO + t)
            act.wait_ge(tl_full, 1)
            for n in range(IN_WT, IN_WT + KT // 2):
                split(n)
            act.wait_ge(fo_out, 16)

            def job(i, c):
                act.wait_ge(job_scaled, i * 4 + (c + 1))
                act.wait_ge(job_stored, i * 64 + 16 * (c + 1))
                A(job_out[:, 0, :], job_in_f, ACT.Copy,
                  scale=up[:, U_JOB + c % 2:U_JOB + c % 2 + 1]).then_inc(job_hi, 1)

            with act.Fori(0, BLOCKS) as i:
                for j in range(NOTS):
                    for m in range(KT):
                        g = G0_NOT + j * 2 * KT + m
                        act.wait_ge(mm_full, i * G_NOT + (g + 1))
                        act.wait_ge(h_split, i * (NOTS * KT) + max(j * KT + m, 1))
                        for dst in (Hb[:, 0, m, :], tmp[:, m % 2, :]):
                            last = A(dst, mm[:, g % RING, :], ACT.Relu, bias=b_not[:, j, m:m + 1],
                                     scale=u[:, V_NOT1 + j:V_NOT1 + j + 1])
                        last.then_inc(act_freed, 1)
                        if m == 4:
                            job(i, 2 * j)
                    act.wait_ge(slot_scaled, i * NOTS + (j + 2))
                    for bt in range(RT):
                        take(R0_NOT + j * RT + bt, 1 - j, bt, U_X + 1 - j, i, R_NOT)
                        act.wait_ge(t_stored[bt % 2], i * (16 * NOTS * RT // 2) + 16 * (1 + j * RT // 2 + bt // 2))
                        for nh in range(2):
                            g = G0_NOT + j * 2 * KT + KT + 2 * bt + nh
                            act.wait_ge(biased, i * (NOTS * KT) + (j * KT + 2 * bt + nh + 1))
                            A(t_out[:, bt % 2, nh * HALF:(nh + 1) * HALF], mm[:, g % RING, :],
                              ACT.Tanh).then_inc(act_freed, 1)
                        if bt == 1:
                            job(i, 2 * j + 1)
            for s in range(2):
                act.wait_ge(t_stored[s], T_STORES)
            act.wait_ge(scaled, 6)
            for n in range(2 * RT):
                take(R0_AND - 2 * RT + n, n // RT, n % RT, U_ALL)
            act.wait_ge(scaled, 7)
            with act.Fori(0, BLOCKS) as i:
                for pair in range(AND_PAIRS):
                    for m in range(KT):
                        g = G0_AND + pair * KT + m
                        act.wait_ge(mm_full, i * G_AND + (g + 1))
                        act.wait_ge(h_split, i * (2 * KT) + (SPLIT_NOT + pair * KT + m - 1))
                        dsts = ((Hb[:, 0, m, :],) if pair == 0 else ()) + (tmp[:, m % 2, :],)
                        for dst in dsts:
                            last = A(dst, mm[:, g % RING, :], ACT.Relu, bias=b_pair[:, 0, m:m + 1],
                                     scale=u_pair[:, m:m + 1])
                        last.then_inc(act_freed, 1)
                        n = pair * 2 * RT + m
                        take(R0_AND + n, 2 * (1 - pair) + m // RT, m % RT, U_ALL, i, R_AND)
                act.wait_ge(and_out, i * 16 + 16)
                for m in range(MT1):
                    g = G0_AND + AND_PAIRS * KT + m
                    act.wait_ge(mm_full, i * G_AND + (g + 1))
                    A(acc[:, m, :], mm[:, g % RING, :], ACT.Copy,
                      scale=u[:, V_TOPA:V_TOPA + 1]).then_inc(act_freed, 1)
                act.wait_ge(act_freed, i * G_AND + (G0_AND + G_AND))
                act.dma_start(and_dram[bass.ds(i * P, P), :],
                              acc[:, :, :].rearrange("p m n -> p (m n)")).then_inc(and_out, 16)
            act.dma_start(Fw[:, :], fo_split).then_inc(fo_in, 16)
            act.dma_start(wt2s, wt2.rearrange("p (k n) -> p k n", k=MT1)).then_inc(top_in, 16)
            act.dma_start(wt1ds, wt1d).then_inc(top_in, 16)
            with act.Fori(0, BLOCKS) as i:
                for m in range(KT):
                    act.wait_ge(mm_full, i * G_OR + (G0_OR + m + 1))
                    if m == 0:
                        act.wait_ge(y_ready, i + 1)
                    act.wait_ge(h_split, i * KT + (SPLIT_AND + m - 1))
                    for dst in (Hb[:, 0, m, :], tmp[:, m % 2, :]):
                        last = A(dst, mm[:, m % RING, :], ACT.Relu, bias=b_pair[:, 1, m:m + 1],
                                 scale=u_pair[:, KT + m:KT + m + 1])
                    last.then_inc(act_freed, 1)
                    if m % 2:
                        take(R0_OR + m // 2, 2, m // 2, U_REM, i, R_OR)
                for m in range(MT1):
                    for n in (2 * m, 2 * m + 1):
                        take(R0_OR + RT + n, n // RT, n % RT, U_ALL, i, R_OR)
                    act.wait_ge(tl_freed, i * T_OR + (m + 2))
                    A(acc[:, m, :], acc[:, m, :], ACT.Relu, bias=c1[:, m:m + 1]).then_inc(h1_ready, 1)
                for m in range(MT2):
                    act.wait_ge(tl_full, i * T_OR + (1 + MT1 + m + 1))
                    A(tmp[:, m, :], tl[:, m % 2, :], ACT.Relu,
                      bias=small[:, S_T2 + m:S_T2 + m + 1]).then_inc(tl_freed, 1)
                act.wait_ge(tl_full, i * T_OR + (1 + T_OR))
                A(acc[0:1, 0, :], tl[0:1, 0, :], ACT.Copy).then_inc(y_ready, 1)
                act.wait_ge(y_ready, i + 2)
                act.sem_inc(tl_freed, 1)

        @block.vector
        def _(dve):
            V = nc.vector
            steps = [0]

            def step(ins, i=None, per=0):
                steps[0] += 1
                ins.then_inc(dve_step, 1)
                dve.wait_ge(dve_step, steps[0] if i is None else i * per + steps[0])

            dve.sem_inc(dve_freed, 2 * MT1)
            dve.sem_inc(tl_freed, 1)
            dve.sem_inc(rem_summed, 1)
            dve.sem_inc(seen_done, 1)
            dve.sem_inc(h_split, 1)
            dve.sem_inc(job_lo, 1)
            dve.sem_inc(y_ready, 1)
            dve.wait_ge(consts_in, 16)
            dve.wait_ge(ints_in, 32)
            at = [TILES * F + F]

            def scratch(*shape):
                n = int(np.prod(shape))
                v = scr[:, at[0]:at[0] + n]
                at[0] += n
                if len(shape) == 2:
                    v = v.rearrange("p (a b) -> p a b", a=shape[0])
                return v

            ids_i = scr[:, 0:TILES * F].bitcast(i32).rearrange("p (t f) -> p t f", f=F)
            fields_i = scr[:, TILES * F:TILES * F + F].bitcast(i32)
            Q = NOTS + SLOTS
            which, neg = scratch(Q), scratch(Q)
            loc, wrap, prod = scratch(TILES, F), scratch(TILES, F), scratch(TILES, F)
            eq, row = scratch(Q, F), scratch(TILES, Q)
            notf, used, rest, valid = scratch(F), scratch(F), scratch(F), scratch(F)
            e6 = scratch(SLOTS, F)
            isn, in0, keep, trow = scratch(SLOTS), scratch(SLOTS), scratch(SLOTS), scratch(SLOTS)
            cnt, e2 = scratch(1), scratch(NOTS, F)
            idxf = scratch(TILES, COLS)
            field_no, start, last_id = (cst[:, k:k + F] for k in (K_FIELD, K_START, K_LAST))
            batch_no = cst[:, K_ROW:K_ROW + TILES]

            def over_tiles(v, n):
                return v.unsqueeze(1).to_broadcast([P, TILES, n])

            step(V.tensor_copy(which, fields_i))
            step(V.tensor_scalar(neg, which, 0.0, float(F), ALU.is_lt, ALU.mult))
            step(V.tensor_tensor(which, which, neg, ALU.add))
            step(V.tensor_copy(loc, ids_i))
            step(V.tensor_scalar(wrap, loc, 0.0, None, ALU.is_lt))
            step(V.tensor_tensor(prod, wrap, over_tiles(last_id, F), ALU.mult))
            step(V.tensor_tensor(loc, loc, prod, ALU.add))
            step(V.tensor_tensor(loc, loc, wrap, ALU.add))
            step(V.tensor_scalar(loc, loc, 0.0, None, ALU.max))
            step(V.tensor_tensor(loc, loc, over_tiles(last_id, F), ALU.min))
            step(V.tensor_tensor(loc, loc, over_tiles(start, F), ALU.add))
            step(V.tensor_tensor(eq, field_no.unsqueeze(1).to_broadcast([P, Q, F]),
                                 which.unsqueeze(2).to_broadcast([P, Q, F]), ALU.is_equal))
            for q in range(Q):
                step(V.tensor_tensor(prod, loc, over_tiles(eq[:, q, :], F), ALU.mult))
                step(V.tensor_reduce(row[:, :, q:q + 1], prod, AX.X, ALU.add))
            step(V.tensor_tensor(notf, eq[:, 0, :], eq[:, 1, :], ALU.max))
            pairs = eq[:, NOTS:Q, :]
            step(V.tensor_tensor(e6, pairs, notf.unsqueeze(1).to_broadcast([P, SLOTS, F]), ALU.mult))
            step(V.tensor_reduce(isn, e6, AX.X, ALU.add))
            step(V.tensor_tensor(e6, pairs, eq[:, 0, :].unsqueeze(1).to_broadcast([P, SLOTS, F]), ALU.mult))
            step(V.tensor_reduce(in0, e6, AX.X, ALU.add))
            step(V.tensor_reduce(used, pairs.rearrange("p q f -> p f q"), AX.X, ALU.max))
            step(V.tensor_scalar(rest, used, -1.0, 1.0, ALU.mult, ALU.add))
            step(V.tensor_reduce(cnt, rest, AX.X, ALU.add))
            step(V.tensor_scalar(cnt, cnt, float(AND_PAIRS + OR_PAIRS), None, ALU.add))
            step(V.reciprocal(invc[:, :], cnt))
            step(V.tensor_copy(idxf[:, :, C_NOT:C_NOT + NOTS], row[:, :, 0:NOTS]))
            step(V.tensor_copy(idxf[:, :, C_ALL:C_ALL + F], loc))

            def masked(cols, n, rows_ap, mask):
                dst = idxf[:, :, cols:cols + n]
                step(V.tensor_scalar(dst, rows_ap, -float(SKIP), None, ALU.add))
                step(V.tensor_tensor(dst, dst, over_tiles(mask, n), ALU.mult))
                step(V.tensor_scalar(dst, dst, float(SKIP), None, ALU.add))

            step(V.tensor_scalar(keep, isn, -1.0, 1.0, ALU.mult, ALU.add))
            masked(C_PX, SLOTS, row[:, :, NOTS:Q], keep)
            step(V.tensor_scalar(trow, in0, -float(B), float(B), ALU.mult, ALU.add))
            tr = idxf[:, :, C_PT:C_PT + SLOTS]
            step(V.tensor_tensor(tr, batch_no.unsqueeze(2).to_broadcast([P, TILES, SLOTS]),
                                 over_tiles(trow, SLOTS), ALU.add))
            masked(C_PT, SLOTS, tr, isn)
            step(V.tensor_scalar(valid, notf, -1.0, 1.0, ALU.mult, ALU.add))
            step(V.tensor_tensor(valid, valid, rest, ALU.mult))
            step(V.tensor_copy(rem_w[:, 0:F], valid))
            step(V.tensor_tensor(e2[:, 0, :], rest, eq[:, 0, :], ALU.mult))
            step(V.tensor_tensor(e2[:, 1, :], rest, eq[:, 1, :], ALU.mult))
            step(V.tensor_scalar(valid, eq[:, 0, :], -1.0, 1.0, ALU.mult, ALU.add))
            step(V.tensor_tensor(e2[:, 1, :], e2[:, 1, :], valid, ALU.mult))
            step(V.tensor_reduce(rem_w[:, F:F + NOTS], e2, AX.X, ALU.add))
            step(V.tensor_copy(idx[:, 0:TILES, :], idxf))
            step(V.tensor_copy(idx[:, TILES:TILES + RT, :], idxf[:, 0:RT, :]))
            for c in (C_PX, C_PT):
                last = V.tensor_copy(idx[:, TILES:TILES + RT, c:c + 2],
                                     idxf[:, 0:RT, c + 2 * AND_PAIRS:c + 2 * AND_PAIRS + 2])
            last.then_inc(idx_ready, 1)

            dve.wait_ge(smalls_in, 16)
            step(V.tensor_scalar(bvec[:, :], small[:, S_A2:S_A2 + KT], float(AND_PAIRS), None, ALU.mult))
            V.scalar_tensor_tensor(out=bvec[:, :], in0=small[:, S_O2:S_O2 + KT], scalar=float(OR_PAIRS),
                                   in1=bvec[:, :], op0=ALU.mult, op1=ALU.add).then_inc(bvec_ready, 1)

            asked = [0]

            def largest(dst, src):
                return V.tensor_reduce(dst, src, AX.X, ALU.max, apply_absolute_value=True)

            def col(t, c):
                return t[:, c:c + 1]

            def scale_from(c, value, i=None, per=0):
                step(V.tensor_scalar(col(down, c), value, LEAST, None, ALU.max), i, per)
                step(V.tensor_scalar(col(down, c).bitcast(i32), col(down, c).bitcast(i32), EXPONENT, None,
                                     ALU.bitwise_and), i, per)
                step(V.tensor_scalar(col(down, c), col(down, c), 2.0 ** -14, None, ALU.mult), i, per)
                step(V.reciprocal(col(up, c), col(down, c)), i, per)

            def sized(c, slices):
                for n, v in enumerate(slices):
                    largest(col(piece, n), v).then_inc(dve_step, 1)
                    steps[0] += 1
                dve.wait_ge(dve_step, steps[0])
                step(V.tensor_reduce(col(part_max, c), piece[:, 0:len(slices)], AX.X, ALU.max))

            def ask():
                asked[0] += 1
                dve.sem_inc(max_asked, 1)

            def f32_slices(v, n):
                return [v[:, s, :, :].rearrange("p h n -> p (h n)").bitcast(fp32) for s in n]

            def split_scale(n):
                return U_N1 if n < IN_N2 else U_N2 if n < IN_FA else U_FA if n < IN_FO else U_FO if n < IN_WT else U_WT

            def lo_in_place(n, v):
                dve.wait_ge(hi_done, n + 1)
                V.scalar_tensor_tensor(out=v[:, 1, :], in0=copied[n % 2], scalar=col(up, split_scale(n)), in1=v[:, 0, :],
                                       op0=ALU.mult, op1=ALU.subtract).then_inc(lo_done, 1)

            for c, k in ((X_BN1, S_N1), (X_BA1, S_A1), (X_BO1, S_O1)):
                step(largest(col(part_max, c), small[:, k:k + KT]))
            dve.wait_ge(wt_in, 16)
            sized(X_WT, f32_slices(Ts, range(KT // 2)))
            dve.wait_ge(wn1_in, 16)
            sized(X_N1, f32_slices(W_not, range(KT)))
            ask()
            dve.wait_ge(max_known, 1)
            scale_from(U_N1, col(all_max, X_N1))
            dve.sem_inc(scaled, 1)
            step(V.tensor_scalar(col(u, V_BOUND), col(all_max, X_N1), float(H), None, ALU.mult))
            dve.wait_ge(wn2_in, 16)
            sized(X_N2, f32_slices(W_not, range(KT, 2 * KT)))
            ask()
            dve.wait_ge(max_known, 2)
            scale_from(U_N2, col(all_max, X_N2))
            dve.sem_inc(scaled, 1)
            def slot_scales(j, i=None, per=0):
                scale_from(U_X + j, col(all_max, X_ROW + j), i, per)
                bound = col(piece, 15)
                step(V.scalar_tensor_tensor(out=bound, in0=col(all_max, X_ROW + j), scalar=col(u, V_BOUND),
                                            in1=col(all_max, X_BN1), op0=ALU.mult, op1=ALU.add), i, per)
                scale_from(U_H + j, bound, i, per)
                step(V.tensor_scalar(b_not[:, j, :], small[:, S_N1:S_N1 + KT], col(up, U_H + j), None, ALU.mult), i, per)
                step(V.scalar_tensor_tensor(out=col(u, V_NOT1 + j), in0=col(up, U_H + j), scalar=col(down, U_X + j),
                                            in1=col(down, U_N1), op0=ALU.mult, op1=ALU.mult), i, per)
                step(V.tensor_tensor(col(u, V_NOT2 + j), col(down, U_H + j), col(down, U_N2), ALU.mult), i, per)
                dve.sem_inc(slot_scaled, 1)

            for t in range(RT):
                dve.wait_ge(not_in[t], 16)
            sized(X_ROW, [not_rows[:, t, :] for t in range(RT)])
            ask()
            dve.wait_ge(max_known, 3)
            slot_scales(0)
            for n in range(2 * KT):
                lo_in_place(n, W_not[:, n, :, :])
            dve.wait_ge(act_freed, KT)
            sized(X_FA, f32_slices(Fs, range(KT // 2)))
            ask()
            dve.wait_ge(max_known, 4)
            scale_from(U_FA, col(all_max, X_FA))
            dve.sem_inc(scaled, 1)
            for n in range(KT // 2):
                lo_in_place(IN_FA + n, Fs[:, n, :, :])

            def take(r, slot, t, scale, i=None, per=0):
                for h in range(2):
                    half = slice(h * KT // 2, (h + 1) * KT // 2)
                    dve.wait_ge(high[h], (r if i is None else i * per + r) + 1)
                    V.scalar_tensor_tensor(out=X[:, slot, 1, half, t * P:(t + 1) * P],
                                           in0=tp[:, h, :].rearrange("p (k b) -> p k b", k=KT // 2),
                                           scalar=col(up, scale),
                                           in1=X[:, slot, 0, half, t * P:(t + 1) * P],
                                           op0=ALU.mult, op1=ALU.subtract).then_inc(taken[h], 1)

            dve.wait_ge(act_freed, G_FOLD)
            sized(X_FO, f32_slices(Fos, range(KT // 2)))
            ask()
            dve.wait_ge(max_known, 5)
            scale_from(U_FO, col(all_max, X_FO))
            scale_from(U_WT, col(all_max, X_WT))
            dve.sem_inc(scaled, 2)
            for t in range(RT):
                take(t, 0, t, U_X)
                lo_in_place(IN_FO + t, Fos[:, t, :, :])
            dve.wait_ge(tl_full, 1)
            V.scalar_tensor_tensor(out=c1[:, :], in0=tl[:, 0, 0:MT1], scalar=invc[:, 0:1],
                                   in1=small[:, S_T1:S_T1 + MT1], op0=ALU.mult, op1=ALU.add).then_inc(c1_ready, 1)
            for n in range(KT // 2):
                lo_in_place(IN_WT + n, Ts[:, n, :, :])
            step(V.memset(field_run[:, :], 1.0))
            dve.wait_ge(bn2_in, 16)
            dve.wait_ge(wt_out, 16)

            def hidden_lo(m, count, i, per):
                dve.wait_ge(act_freed, i * per + count)
                V.tensor_tensor(Hb[:, 1, m, :], tmp[:, m % 2, :], Hb[:, 0, m, :], ALU.subtract).then_inc(h_split, 1)

            def see(i, n):
                dve.wait_ge(seen_in[n % 2], i * (16 * SEEN // 2) + 16 * (n // 2 + 1))
                largest(col(piece, n % (SEEN // NOTS)) if n % (SEEN // NOTS) < 15 else col(field_run, 1),
                        seen[n % 2])
                t, f = n // F, n % F
                total = rem_acc[:, t % 2, :]
                if f == 0:
                    dve.wait_ge(rem_stored[t % 2], i * (16 * RT // 2) + 16 * (1 + t // 2))
                    V.tensor_scalar(total, seen[n % 2], col(rem_w, f), None, ALU.mult).then_inc(seen_done, 1)
                else:
                    dve.wait_ge(seen_done, i * SEEN + (n + 1))
                    V.scalar_tensor_tensor(out=total, in0=seen[n % 2], scalar=col(rem_w, f), in1=total,
                                           op0=ALU.mult, op1=ALU.add).then_inc(seen_done, 1)

            base = steps[0]
            PER = NOT_STEPS
            with dve.Fori(0, BLOCKS) as i:
                for j in range(NOTS):
                    def ask_for(k):
                        dve.sem_inc(max_asked, 1)

                    def known(k):
                        dve.wait_ge(max_known, i * (3 * NOTS) + (5 + 3 * j + k + 1))

                    def job_max(c):
                        dve.wait_ge(job_read, i * 64 + 16 * (c + 1))
                        step(largest(col(part_max, X_JOB + c % 2), job_in_f), i, PER)
                        ask_for(2 * (c % 2))

                    def job_scale(c):
                        known(2 * (c % 2))
                        scale_from(U_JOB + c % 2, col(all_max, X_JOB + c % 2), i, PER)
                        step(V.tensor_copy(slice_max[:, bass.ds(i * 4 + c, 1)], col(all_max, X_JOB + c % 2)), i, PER)
                        step(V.tensor_copy(slice_down[:, bass.ds(i * 4 + c, 1)], col(down, U_JOB + c % 2)), i, PER)
                        dve.sem_inc(job_scaled, 1)

                    def job_rest(c):
                        dve.wait_ge(job_hi, i * 4 + (c + 1))
                        V.scalar_tensor_tensor(out=job_out[:, 1, :], in0=job_in_f, scalar=col(up, U_JOB + c % 2),
                                               in1=job_out[:, 0, :], op0=ALU.mult, op1=ALU.subtract).then_inc(job_lo, 1)

                    for m in range(KT):
                        hidden_lo(m, G0_NOT + j * 2 * KT + m + 1, i, G_NOT)
                        if m == 2:
                            job_max(2 * j)
                        if m == 3:
                            job_scale(2 * j)
                        if m == 4:
                            job_rest(2 * j)
                        if m in (0, 1, 3, 6):
                            t = (0, 1, 3, 6).index(m)
                            dve.wait_ge(not_in[t], i * (16 * NOTS) + 16 * (j + 2))
                            step(largest(col(rowmax, t), not_rows[:, t, :]), i, PER)
                        if m == 6:
                            step(V.tensor_reduce(col(part_max, X_ROW + 1 - j), rowmax[:, 0:RT], AX.X, ALU.max), i, PER)
                            ask_for(1)
                        if m == 7:
                            known(1)
                            slot_scales(1 - j, i, PER)
                        if m < SEEN_FIRST:
                            see(i, j * (SEEN // NOTS) + m)
                    for bt in range(RT):
                        take(R0_NOT + j * RT + bt, 1 - j, bt, U_X + 1 - j, i, R_NOT)
                        if bt == 2:
                            job_rest(2 * j + 1)
                        for nh in range(2):
                            g = G0_NOT + j * 2 * KT + KT + 2 * bt + nh
                            dve.wait_ge(mm_full, i * G_NOT + (g + 1))
                            V.scalar_tensor_tensor(out=mm[:, g % RING, :], in0=mm[:, g % RING, :],
                                                   scalar=col(u, V_NOT2 + j), in1=bnb[:, nh * HALF:(nh + 1) * HALF],
                                                   op0=ALU.mult, op1=ALU.add).then_inc(biased, 1)
                            see(i, j * (SEEN // NOTS) + SEEN_FIRST + 2 * bt + nh + max(bt - 1, 0))
                        if bt == 0:
                            job_max(2 * j + 1)
                        if bt == 1:
                            job_scale(2 * j + 1)
                        if bt:
                            see(i, j * (SEEN // NOTS) + SEEN_FIRST + 3 * bt + 1)
                    dve.wait_ge(seen_done, i * SEEN + (1 + (j + 1) * (SEEN // NOTS)))
                    step(V.tensor_reduce(col(part_max, X_ALL), piece[:, 0:SEEN // NOTS - 1], AX.X, ALU.max), i, PER)
                    step(V.tensor_tensor(col(part_max, X_ALL), col(part_max, X_ALL), col(field_run, 1), ALU.max), i, PER)
                    step(V.tensor_tensor(col(field_run, 0), col(field_run, 0), col(part_max, X_ALL), ALU.max), i, PER)
            assert steps[0] - base == NOT_STEPS, steps[0] - base
            steps[0] = base + BLOCKS * NOT_STEPS

            step(V.tensor_copy(col(part_max, X_ALL), col(field_run, 0)))
            dve.sem_inc(max_asked, 1)
            dve.wait_ge(max_known, 5 + 3 * NOTS * BLOCKS + 1)
            x_all = col(all_max, X_ALL)
            scale_from(U_ALL, x_all)
            dve.sem_inc(scaled, 1)
            for n in range(2 * RT):
                take(R0_AND - 2 * RT + n, n // RT, n % RT, U_ALL)
            for c, bias, k, pairs_n, s in ((U_RA, X_BA1, 0, AND_PAIRS, S_A1), (U_RO, X_BO1, 1, OR_PAIRS, S_O1)):
                bound = col(rowmax, 0)
                step(V.tensor_reduce(bound, slice_max[:, k * KT:(k + 1) * KT], AX.X, ALU.max))
                step(V.tensor_scalar(bound, bound, x_all, float(2 * H), ALU.mult, ALU.mult))
                step(V.tensor_tensor(bound, bound, col(all_max, bias), ALU.add))
                step(V.tensor_scalar(bound, bound, float(pairs_n), None, ALU.mult))
                scale_from(c, bound)
                step(V.tensor_scalar(b_pair[:, k, :], small[:, s:s + KT], col(up, c), None, ALU.mult))
                step(V.tensor_scalar(u_pair[:, k * KT:(k + 1) * KT], slice_down[:, k * KT:(k + 1) * KT],
                                     col(down, U_ALL), col(up, c), ALU.mult, ALU.mult))
            step(V.tensor_scalar(col(rowmax, 0), x_all, float(F), None, ALU.mult))
            scale_from(U_REM, col(rowmax, 0))
            for dst, a, b in ((V_TOPA, U_RA, U_FA), (V_TOPO, U_RO, U_FO), (V_TOPR, U_REM, U_WT)):
                step(V.tensor_tensor(col(u, dst), col(down, a), col(down, b), ALU.mult))
            dve.sem_inc(scaled, 1)

            with dve.Fori(0, BLOCKS) as i:
                for pair in range(AND_PAIRS):
                    for m in range(KT):
                        g = G0_AND + pair * KT + m
                        if pair == 0:
                            hidden_lo(m, g + 1, i, G_AND)
                        else:
                            t, p0 = tmp[:, m % 2, :], 3 * m
                            dve.wait_ge(act_freed, i * G_AND + (g + 1))
                            V.tensor_tensor(t, t, Hb[:, 0, m, :], ALU.add).then_inc(pair_step, 1)
                            dve.wait_ge(pair_step, i * (3 * KT) + (p0 + 1))
                            V.tensor_tensor(t, t, Hb[:, 1, m, :], ALU.add).then_inc(pair_step, 1)
                            dve.wait_ge(pair_step, i * (3 * KT) + (p0 + 2))
                            V.tensor_copy(Hb[:, 0, m, :], t).then_inc(pair_step, 1)
                            dve.wait_ge(pair_step, i * (3 * KT) + (p0 + 3))
                            V.tensor_tensor(Hb[:, 1, m, :], t, Hb[:, 0, m, :], ALU.subtract).then_inc(h_split, 1)
                        take(R0_AND + pair * 2 * RT + m, 2 * (1 - pair) + m // RT, m % RT, U_ALL, i, R_AND)

            dve.wait_ge(c1_ready, 1)
            with dve.Fori(0, BLOCKS) as i:
                for m in range(KT):
                    hidden_lo(m, G0_OR + m + 1, i, KT)
                    if m % 2 == 0:
                        t = m // 2
                        dve.wait_ge(rem_in, i * (16 * RT) + 16 * (t + 1))
                        for j in range(NOTS):
                            dve.wait_ge(rem_t_in[j], i * (16 * RT) + 16 * (t + 1))
                            V.scalar_tensor_tensor(out=rem_sum, in0=rem_t[j], scalar=col(rem_w, F + j), in1=rem_sum,
                                                   op0=ALU.mult, op1=ALU.add).then_inc(rem_step, 1)
                            dve.wait_ge(rem_step, i * (NOTS * RT) + (NOTS * t + j + 1))
                        dve.sem_inc(rem_summed, 1)
                    else:
                        take(R0_OR + m // 2, 2, m // 2, U_REM, i, R_OR)
                dve.wait_ge(and_in, i * 16 + 16)
                for m in range(MT1):
                    for q, c in enumerate((V_TOPR, V_TOPO)):
                        n = 2 * m + q
                        dve.wait_ge(mm_full, i * G_OR + (G0_OR + KT + n + 1))
                        V.scalar_tensor_tensor(out=acc[:, m, :], in0=mm[:, n % RING, :], scalar=col(u, c),
                                               in1=acc[:, m, :], op0=ALU.mult, op1=ALU.add).then_inc(acc_step, 1)
                        dve.wait_ge(acc_step, i * (3 * MT1) + (3 * m + q + 1))
                        dve.sem_inc(dve_freed, 1)
                        if q == 0:
                            take(R0_OR + RT + n, n // RT, n % RT, U_ALL, i, R_OR)
                    dve.wait_ge(tl_full, i * T_OR + (1 + m + 1))
                    V.scalar_tensor_tensor(out=acc[:, m, :], in0=acc[:, m, :], scalar=invc[:, 0:1],
                                           in1=tl[:, m % 2, :], op0=ALU.mult, op1=ALU.add).then_inc(acc_step, 1)
                    dve.wait_ge(acc_step, i * (3 * MT1) + (3 * m + 3))
                    dve.sem_inc(tl_freed, 1)
                    n = 2 * m + 1
                    take(R0_OR + RT + n, n // RT, n % RT, U_ALL, i, R_OR)


def weight_slices(w):
    k, m = w.shape
    return np.ascontiguousarray(w.reshape(k // P, P, m // P, P).transpose(2, 1, 0, 3)).reshape(m // P, P, k)


def by_partition(w):
    k, n = w.shape
    return np.ascontiguousarray(w.reshape(k // P, P, n).transpose(1, 0, 2)).reshape(P, k // P * n)


def kernel(**inputs):
    import concourse.bacc as bacc
    from concourse.bass_utils import run_bass_kernel_spmd

    a = {k: np.asarray(v) for k, v in inputs.items()}
    consts = np.zeros((P, K_COLS), np.float32)
    consts[:, K_FIELD:K_FIELD + F] = np.arange(F)
    consts[:, K_START:K_START + F] = TABLE_START
    consts[:, K_LAST:K_LAST + F] = [n - 1 for n in TABLE_ROWS]
    consts[:, K_ROW:K_ROW + TILES] = np.arange(B).reshape(TILES, P).T
    consts[:, K_IDENT:] = np.eye(P)
    w_top1, w_z = a["W_top1"], a["W_top1"][:H]
    names = ["L0_rec_bn1", "L0_rec_ba1", "L0_rec_bo1", "L0_rec_ba2", "L0_rec_bo2", "b_top1", "b_top2"]
    smalls = [a[n].reshape(-1, P).T for n in names] + [a["W_top3"].reshape(MT2, P).T]
    n1 = weight_slices(a["L0_rec_Wn1"])
    data = {
        "table": np.concatenate([a[f"tbl_{f}"] for f in range(F)], axis=0),
        "ids": np.ascontiguousarray(a["ids"].reshape(TILES, P, F).transpose(1, 0, 2)).reshape(P, TILES * F),
        "fields": np.concatenate([a["L0_rec_not_idx"].reshape(-1), a["L0_rec_and_pairs"].reshape(-1),
                                  a["L0_rec_or_pairs"].reshape(-1)]),
        "consts": consts,
        "smalls": np.ascontiguousarray(np.concatenate(smalls, axis=1)),
        "bn2": a["L0_rec_bn2"],
        "wn1": np.ascontiguousarray(n1.transpose(1, 0, 2)).reshape(P, KT * H),
        "wn2": by_partition(a["L0_rec_Wn2"]),
        "pair_w": np.concatenate([weight_slices(a["L0_rec_Wa1"]), weight_slices(a["L0_rec_Wo1"])]),
        "w2ta": weight_slices(a["L0_rec_Wa2"].T),
        "w2to": weight_slices(a["L0_rec_Wo2"].T),
        "wt1": by_partition(w_z),
        "wt1d": np.ascontiguousarray(w_top1[H:]),
        "wt2": by_partition(a["W_top2"]),
        "dense_t": np.ascontiguousarray(a["dense_ctx"].T),
    }
    nc = bacc.Bacc("TRN2", target_bir_lowering=False, num_devices=1)
    args = {k: nc.dram_tensor(f"in_{k}", v.shape, mybir.dt.from_np(v.dtype), kind="ExternalInput").ap()
            for k, v in data.items()}
    y = nc.dram_tensor("y", (B, 1), mybir.dt.float32, kind="ExternalOutput").ap()
    build(nc, **args, out=y)
    r = run_bass_kernel_spmd(nc, [{f"in_{k}": v for k, v in data.items()}], core_ids=[0])
    return r.results[0]["y"]
```
